# Optimizing a Trainium2 kernel written in Bass

```python
import numpy as np
import jax
import jax.numpy as jnp

def _softmax(x, axis=-1):
    return jax.nn.softmax(x, axis=axis)

def _gelu(x):
    return jax.nn.gelu(x, approximate=True)

def _silu(x):
    return jax.nn.silu(x)

def _sigmoid(x):
    return jax.nn.sigmoid(x)

def _layernorm(x, axis=-1, eps=1e-05):
    m = jnp.mean(x, axis=axis, keepdims=True)
    v = jnp.var(x, axis=axis, keepdims=True)
    return (x - m) / jnp.sqrt(v + eps)

def _scatter_add(tgt, idx, src, axis=0):
    return tgt.at[idx].add(src)

def _segment_sum(src, seg, n):
    return jax.ops.segment_sum(src, seg, n)
kernel_name = 'mk_flamingo_gated_d1_seqx_r2_40905b'

def setup_inputs(seed: int=0):
    np.random.seed(seed)
    _w = jnp.asarray

    def _rec_inputs():
        import jax
        import jax.numpy as jnp
        _rk = jax.random.key(seed)
        x = -0.0002928 + 1 * jax.random.normal(jax.random.fold_in(_rk, 1), (4, 2048, 512), jnp.float32)
        _lenS = 2048 - jax.random.randint(jax.random.fold_in(_rk, 7), (4,), 0, max(1, 2048 // 4) + 1, jnp.int32)
        _lenS2 = 154 - jax.random.randint(jax.random.fold_in(_rk, 8), (4,), 0, max(1, 154 // 4) + 1, jnp.int32)
        _ctx_1024P = jax.random.normal(jax.random.fold_in(_rk, 11), (4, 16, 512), jnp.float32)
        _ctx_1024c = jax.random.dirichlet(jax.random.fold_in(_rk, 511), 0.3 * jnp.ones((16,), jnp.float32), (4, 154))
        _ctx_1024t = jnp.einsum('bsk,bkd->bsd', _ctx_1024c, _ctx_1024P)
        _ctx_1024t = _ctx_1024t * jax.lax.rsqrt(jnp.mean(jnp.square(_ctx_1024t)) + 1e-12) * 0.953939
        ctx_1024 = 4.13588e-05 + 0.999923 * (_ctx_1024t + 0.3 * jax.random.normal(jax.random.fold_in(_rk, 611), (4, 154, 512), jnp.float32))
        _g = jax.random.normal(jax.random.fold_in(_rk, 9001), (2, 1), jnp.float32)
        _g = jnp.sign(_g) * jnp.maximum(jnp.abs(_g), 1.0) + (_g == 0) * 1.0
        g_xattn = _g[0]
        g_ffn = _g[1]
        return (x, ctx_1024, g_xattn, g_ffn)
    x, ctx_1024, g_xattn, g_ffn = _rec_inputs()

    def _L0_xattn_setup():
        import jax, jax.numpy as jnp
        import numpy as np
        D_MODEL = 512
        N_HEADS = 16
        D_HEAD = D_MODEL // N_HEADS
        key = jax.random.key(seed)
        ks = jax.random.split(key, 6)
        query = jax.random.normal(ks[0], (2, 1024, D_MODEL), dtype=jnp.float32)
        context = jax.random.normal(ks[1], (2, 2048, D_MODEL), dtype=jnp.float32)
        s = 1.0 / np.sqrt(D_MODEL)
        Wq = jax.random.normal(ks[2], (D_MODEL, D_MODEL), dtype=jnp.float32) * s
        Wk = jax.random.normal(ks[3], (D_MODEL, D_MODEL), dtype=jnp.float32) * s
        Wv = jax.random.normal(ks[4], (D_MODEL, D_MODEL), dtype=jnp.float32) * s
        Wo = jax.random.normal(ks[5], (D_MODEL, D_MODEL), dtype=jnp.float32) * s
        return {'query': query, 'context': context, 'Wq': Wq, 'Wk': Wk, 'Wv': Wv, 'Wo': Wo}
    _L0_xattn_all = _L0_xattn_setup()
    _L0_xattn_in = {k: v for k, v in _L0_xattn_all.items() if k in ('Wq', 'Wk', 'Wv', 'Wo')}
    del _L0_xattn_all

    def _L0_ffn_setup():
        import jax, jax.numpy as jnp
        import numpy as np
        DIM = 512

        def _reference_tuple_inner(x, W_r, W_k, W_v, mu_r, mu_k):
            B, T, C = x.shape
            x_prev = jnp.concatenate([jnp.zeros((B, 1, C), x.dtype), x[:, :-1, :]], axis=1)
            xr = mu_r * x + (1.0 - mu_r) * x_prev
            xk = mu_k * x + (1.0 - mu_k) * x_prev
            r = jax.nn.sigmoid(jnp.einsum('btc,dc->btd', xr, W_r))
            k = jnp.einsum('btc,dc->btd', xk, W_k)
            k_act = jnp.square(jax.nn.relu(k))
            out = r * jnp.einsum('btc,dc->btd', k_act, W_v)
            new_state = x[:, -1, :]
            return (out, new_state)
        key = jax.random.key(seed)
        ks = jax.random.split(key, 6)
        B, T, C = (8, 1024, DIM)
        x = jax.random.normal(ks[0], (B, T, C), dtype=jnp.float32)
        s = 1.0 / np.sqrt(C)
        W_r = jax.random.uniform(ks[1], (C, C), jnp.float32, -s, s)
        W_k = jax.random.uniform(ks[2], (C, C), jnp.float32, -s, s)
        W_v = jax.random.uniform(ks[3], (C, C), jnp.float32, -s, s)
        mu_r = jax.random.uniform(ks[4], (C,), jnp.float32)
        mu_k = jax.random.uniform(ks[5], (C,), jnp.float32)
        return {'x': x, 'W_r': W_r, 'W_k': W_k, 'W_v': W_v, 'mu_r': mu_r, 'mu_k': mu_k}
    _L0_ffn_all = _L0_ffn_setup()
    _L0_ffn_in = {k: v for k, v in _L0_ffn_all.items() if k in ('W_r', 'W_k', 'W_v', 'mu_r', 'mu_k')}
    del _L0_ffn_all
    return {'x': x, 'ctx_1024': ctx_1024, 'g_xattn': g_xattn, 'g_ffn': g_ffn, 'L0_xattn_Wq': _L0_xattn_in['Wq'], 'L0_xattn_Wk': _L0_xattn_in['Wk'], 'L0_xattn_Wv': _L0_xattn_in['Wv'], 'L0_xattn_Wo': _L0_xattn_in['Wo'], 'L0_ffn_W_r': _L0_ffn_in['W_r'], 'L0_ffn_W_k': _L0_ffn_in['W_k'], 'L0_ffn_W_v': _L0_ffn_in['W_v'], 'L0_ffn_mu_r': _L0_ffn_in['mu_r'], 'L0_ffn_mu_k': _L0_ffn_in['mu_k']}

def reference(x, ctx_1024, g_xattn, g_ffn, L0_xattn_Wq, L0_xattn_Wk, L0_xattn_Wv, L0_xattn_Wo, L0_ffn_W_r, L0_ffn_W_k, L0_ffn_W_v, L0_ffn_mu_r, L0_ffn_mu_k):
    import jax
    import jax.numpy as jnp

    def _L0_xattn_ref(query, context, Wq, Wk, Wv, Wo):
        import jax, jax.numpy as jnp
        import numpy as np
        D_MODEL = 512
        N_HEADS = 16
        D_HEAD = D_MODEL // N_HEADS
        B, T_q, D = query.shape
        T_c = context.shape[1]
        Q = (query @ Wq.T).reshape(B, T_q, N_HEADS, D_HEAD)
        K = (context @ Wk.T).reshape(B, T_c, N_HEADS, D_HEAD)
        V = (context @ Wv.T).reshape(B, T_c, N_HEADS, D_HEAD)
        scale = jnp.sqrt(jnp.asarray(D_HEAD, dtype=query.dtype))
        scores = jnp.einsum('bqhd,bkhd->bhqk', Q, K) / scale
        attn = jax.nn.softmax(scores, axis=-1)
        out = jnp.einsum('bhqk,bkhd->bqhd', attn, V).reshape(B, T_q, D)
        return out @ Wo.T

    def _L0_ffn_ref(x, W_r, W_k, W_v, mu_r, mu_k):
        import jax, jax.numpy as jnp
        import numpy as np
        DIM = 512

        def _reference_tuple_inner(x, W_r, W_k, W_v, mu_r, mu_k):
            B, T, C = x.shape
            x_prev = jnp.concatenate([jnp.zeros((B, 1, C), x.dtype), x[:, :-1, :]], axis=1)
            xr = mu_r * x + (1.0 - mu_r) * x_prev
            xk = mu_k * x + (1.0 - mu_k) * x_prev
            r = jax.nn.sigmoid(jnp.einsum('btc,dc->btd', xr, W_r))
            k = jnp.einsum('btc,dc->btd', xk, W_k)
            k_act = jnp.square(jax.nn.relu(k))
            out = r * jnp.einsum('btc,dc->btd', k_act, W_v)
            new_state = x[:, -1, :]
            return (out, new_state)
        return _reference_tuple_inner(x, W_r, W_k, W_v, mu_r, mu_k)[0]
    x = x + jnp.tanh(g_xattn[0]) * _L0_xattn_ref(_layernorm(x, axis=-1), ctx_1024, L0_xattn_Wq, L0_xattn_Wk, L0_xattn_Wv, L0_xattn_Wo)
    x = x + jnp.tanh(g_ffn[0]) * _L0_ffn_ref(_layernorm(x, axis=-1), L0_ffn_W_r, L0_ffn_W_k, L0_ffn_W_v, L0_ffn_mu_r, L0_ffn_mu_k)
    return x

_drawn_inputs = setup_inputs


def setup_inputs(seed=0):
    import zlib

    import numpy as np

    out = dict(_drawn_inputs(seed))
    spreads = {}
    factors = {'L0_ffn_W_r': 3.328, 'L0_ffn_mu_r': 7.489}
    for name, (base, spread) in spreads.items():
        noise = np.random.default_rng([zlib.crc32(name.encode()), seed]).standard_normal(out[name].shape)
        drawn = base * np.exp(spread * noise) if base else spread * noise
        out[name] = jnp.asarray(drawn.astype(out[name].dtype))
    for name, factor in factors.items():
        out[name] = (out[name] * factor).astype(out[name].dtype)
    return out
```

```python
from contextlib import ExitStack

import concourse.bass as bass
from concourse import mybir

F32 = mybir.dt.float32
F32R = mybir.dt.float32r
F16 = mybir.dt.float16
ALU = mybir.AluOpType
ACT = mybir.ActivationFunctionType
AX = mybir.AxisListType

HI, LO = 0, 1
PRODUCTS = ((HI, HI), (HI, LO), (LO, HI))


def flamingo_block(nc, x, ctx_tokens, g_xattn, g_ffn, Wq, Wk, Wv, Wo, W_r, W_k, W_v, mu_r, mu_k, out):
    B, T, D = x.shape
    S = ctx_tokens.shape[1]
    H = 16
    DH = D // H
    P = 128
    C = D // P
    G = H // 4
    N = 512
    TT = N // P
    BLOCKS = B * T // N
    PER_BATCH = T // N
    TAIL = 32
    OVER = P + TAIL - S
    SCALE = float(DH) ** -0.5
    EPS = 1e-5
    assert D == C * P == 512 and DH == 32 and C == G == TT and P < S <= P + TAIL and T % N == 0

    x_tiles = x.rearrange("b (n t p) d -> (b n) t p d", t=TT, p=P)
    out_tiles = out.rearrange("b (n t p) d -> (b n) t p d", t=TT, p=P)

    k_scratch = nc.dram_tensor("k_scratch", [B, P, 2, G, 2 * P], F32, kind="Internal").ap()
    v_scratch = nc.dram_tensor("v_scratch", [B, P, 2, D], F16, kind="Internal").ap()
    vt_scratch = nc.dram_tensor("vt_scratch", [B, TAIL, 2, D], F16, kind="Internal").ap()

    with ExitStack() as ctx:
        def sb(name, shape, dt):
            return ctx.enter_context(nc.sbuf_tensor(name, shape, dt))

        def psum(name):
            return ctx.enter_context(nc.psum_tensor(name, [P, 512], F32))

        def sem(name):
            return ctx.enter_context(nc.semaphore(name))

        WqT, WoT, WrT, WkT2, WvT2 = (sb(n, [P, 2, C, D], F32R) for n in ("WqT", "WoT", "WrT", "WkT2", "WvT2"))
        buf1 = sb("buf1", [P, 2, C, N], F32R)
        buf2 = sb("buf2", [P, 2, C, N], F32R)
        buf3 = sb("buf3", [P, 2, C, N], F32R)
        buf4 = sb("buf4", [P, 2, C, N], F32R)
        k_pad = sb("k_pad", [P, 2, G, 4, P], F32R)
        k_tail = sb("k_tail", [P, 2, G, 4, TAIL], F32R)
        v_main = sb("v_main", [P, 2, D], F16)
        v_tail = sb("v_tail", [P, 2, G, 4, TAIL], F16)
        ones_main = sb("ones_main", [P, DH], F16)
        ones_tail = sb("ones_tail", [P, 4, DH], F16)
        xa = sb("xa", [P, 3, D], F32)
        x1 = sb("x1", [P, TT, D], F32)
        ring = sb("ring", [P, C * (N + 1) + 2 * N], F32)
        tmp = sb("tmp", [P, 2, N], F32)
        th = sb("th", [P, N], F32)
        mm = sb("mm", [P, TT, P], F32)
        mT = sb("mT", [P, N], F32R)
        mx = sb("mx", [P, TT, H], F32)
        ident = sb("ident", [P, P], F32)
        negsel = sb("negsel", [P, H, TAIL], F32R)
        mask = sb("mask", [P, 1], F32)
        minus_half = sb("minus_half", [P, 1], F32)
        flag = sb("flag", [P, BLOCKS], F32)
        carry = sb("carry", [P, C], F32)
        mu = sb("mu", [P, 2, C], F32)
        gate = sb("gate", [P, 4], F32)
        gate_tanh = sb("gate_tanh", [P, 2], F32)
        stats = sb("stats", [P, 2, TT, 6], F32)
        mv = sb("mv", [P, 2, TT, 2], F32)
        nm = sb("nm", [P, 2, TT], F32)
        ve = sb("ve", [P, 2, TT], F32)
        rstd = sb("rstd", [P, 2, TT], F32)
        nb = sb("nb", [P, 2, TT], F32)
        eps = sb("eps", [P, 1], F32)

        p32 = (ring[:, 0:N], tmp[:, 1, :])
        pq = ring[:, N:6 * N].bitcast(F16).rearrange("p (c s n) -> p c s n", c=5, s=2)
        X2W = N + 1
        x2 = ring[:, 0:C * X2W].rearrange("p (c n) -> p c n", c=C)
        k2 = (tmp[:, 0, :], th[:, :])
        mixed = [ring[:, C * X2W + N * n:C * X2W + N * (n + 1)] for n in range(2)]
        diff = (th[:, :], xa[:, 1, :], xa[:, 2, :], tmp[:, 1, :])

        s_bank = [psum(f"s_bank{n}") for n in range(3)]
        o_bank, d_bank = psum("o_bank"), psum("d_bank")
        g_bank = [psum(f"g_bank{n}") for n in range(3)]

        consts_ready = sem("consts_ready")
        chain = {n: sem(f"chain_{n}") for n in ("pool", "act")}
        small_loaded = sem("small_loaded")
        gates_ready = sem("gates_ready")
        nat_loaded = [sem("nat_loaded0"), sem("nat_loaded1")]
        w_transposed = sem("w_transposed")
        w_hi = sem("w_hi")
        w_lo = sem("w_lo")
        ctx_loaded = sem("ctx_loaded")
        ctx_transposed = sem("ctx_transposed")
        ctx_hi = sem("ctx_hi")
        ctx_lo = sem("ctx_lo")
        kv_done = sem("kv_done")
        kv_hi = sem("kv_hi")
        kv_lo = sem("kv_lo")
        kv_stored = sem("kv_stored")
        kv_loaded = sem("kv_loaded")
        xa_loaded = [sem(f"xa_loaded{t}") for t in range(TT)]
        x1_loaded = [sem(f"x1_loaded{t}") for t in range(TT)]
        out_stored = [sem(f"out_stored{t}") for t in range(TT)]
        bn_ready, sum_ready, aggr_ready, mean_ready, var_eps_ready, rstd_ready, norm_ready = (
            [sem(f"{n}{which}") for which in (1, 2)]
            for n in ("bn_ready", "sum_ready", "aggr_ready", "mean_ready", "var_eps_ready", "rstd_ready", "norm_ready"))
        dve_small = sem("dve_small")
        xn1_ready = sem("xn1_ready")
        xn2_ready = sem("xn2_ready")
        xT_done, xT_hi, xT_lo = sem("xT_done"), sem("xT_hi"), sem("xT_lo")
        q_done, q_hi, q_copied, q_lo = sem("q_done"), sem("q_hi"), sem("q_copied"), sem("q_lo")
        max_done = sem("max_done")
        reduced = sem("reduced")
        mm_ready, mT_done, mT_ready = sem("mm_ready"), sem("mT_done"), sem("mT_ready")
        scores_done = sem("scores_done")
        p_hi, p_full, p_lo = sem("p_hi"), sem("p_full"), sem("p_lo")
        av_done = sem("av_done")
        recip_ready, attn32_ready = sem("recip_ready"), sem("attn32_ready")
        attn_hi, attn_lo = sem("attn_hi"), sem("attn_lo")
        wo_done, x1_ready = sem("wo_done"), sem("x1_ready")
        x2_done, x2_ready = sem("x2_done"), sem("x2_ready")
        x2_first, carry_ready = sem("x2_first"), sem("carry_ready")
        diff_ready = sem("diff_ready")
        xk_mixed, xk_hi, xk_lo = sem("xk_mixed"), sem("xk_hi"), sem("xk_lo")
        xr_mixed, xr_hi, xr_lo = sem("xr_mixed"), sem("xr_hi"), sem("xr_lo")
        k_done, relu_ready, k2_ready, k2_hi, k2_lo = (sem(n) for n in ("k_done", "relu_ready", "k2_ready", "k2_hi", "k2_lo"))
        r_done, th_ready, v_done, u_ready, out_ready = (sem(n) for n in ("r_done", "th_ready", "v_done", "u_ready", "out_ready"))
        XT_BANK, WO_BANK, Q_BANK = (0, 1, 2, 0), (0, 1, 2, 1), (2, 0, 1, 2)
        K_BANK, R_BANK, V_BANK = (0, 1, 2, 0), (1, 0, 2, 1), (2, 1, 0, 2)
        SCORE_UNITS, MAX_UNITS = G * 5, TT * G + TT
        score_bank = [s_bank[(m + 1) % 3] for m in range(SCORE_UNITS)]
        max_bank = [s_bank[(SCORE_UNITS + n) % 3] for n in range(MAX_UNITS)]
        x2_bank = [(o_bank, d_bank)[t % 2] for t in range(TT)]
        mT_bank = o_bank
        KV_LOADS = 13

        weights = (("wk", Wk, buf1), ("wv", Wv, buf2), ("wq", Wq, WqT), ("wk2", W_k, WkT2), ("wr", W_r, WrT),
                   ("wv2", W_v, WvT2), ("wo", Wo, WoT))
        nat = (x1, ring[:, 0:C * D].rearrange("p (c n) -> p c n", c=C))

        block = ctx.enter_context(nc.Block())

        def later(eng, semaphore, value):
            if not isinstance(value, int) or value > 0:
                eng.wait_ge(semaphore, value)

        @block.sync
        def _(sp):
            for col, g in enumerate((g_xattn, g_ffn)):
                sp.dma_start(gate[:, col:col + 1], g.rearrange("(a n) -> a n", a=1).to_broadcast([P, 1])).then_inc(small_loaded, 16)
            for n, m in enumerate((mu_r, mu_k)):
                sp.dma_start(mu[:, n, :], m.rearrange("(c p) -> p c", p=P), allow_slow_non_contiguous=True).then_inc(small_loaded, 16)
            for n, (_, w, _) in enumerate(weights):
                if n >= 2:
                    sp.wait_ge(w_transposed, C * (n - 1))
                sp.dma_start(nat[n % 2][:, :, :], w.rearrange("(o p) i -> p o i", p=P)).then_inc(nat_loaded[n % 2], 16)
            def batch_in(b):
                later(sp, ctx_transposed, b * 2)
                sp.dma_start(xa[:, 0, :], ctx_tokens[b, 0:P, :]).then_inc(ctx_loaded, 16)
                sp.dma_start(xa[:, 1, :], ctx_tokens[b, S - P:S, :]).then_inc(ctx_loaded, 16)
                sp.wait_ge(kv_lo, b * (G + 2) + G + 2)
                sp.wait_ge(kv_hi, b * (G + 2) + G + 2)
                sp.dma_start(k_scratch[b], buf4[:, :, :, 0:2 * P].bitcast(F32)).then_inc(kv_stored, 16)
                sp.dma_start(v_scratch[b], tmp[:, 0, :].bitcast(F16).rearrange("p (s n) -> p s n", s=2)).then_inc(kv_stored, 16)
                sp.dma_start(vt_scratch[b], tmp[P - TAIL:P, 1, :].bitcast(F16).rearrange("p (s n) -> p s n", s=2)).then_inc(kv_stored, 16)

            batch_in(0)
            with sp.Fori(1, B) as b:
                batch_in(b)

            def load_xa(i, t):
                sp.dma_start(xa[:, t % 3, :], x_tiles[i, t]).then_inc(xa_loaded[t], 16)

            def load_x1(i, t):
                later(sp, out_stored[t], 16 * i)
                sp.dma_start(x1[:, t, :], x_tiles[i, t]).then_inc(x1_loaded[t], 16)

            def load_kv(i):
                later(sp, av_done, i * G)
                b = i // PER_BATCH
                for j in range(4):
                    rows = slice(DH * j, DH * j + DH)
                    sp.dma_start(k_pad[rows, :, :, j, :].bitcast(F32), k_scratch[b, rows, :, :, 0:P]).then_inc(kv_loaded, 16)
                    sp.dma_start(k_tail[rows, :, :, j, :].bitcast(F32), k_scratch[b, rows, :, :, 2 * P - TAIL:2 * P]).then_inc(kv_loaded, 16)
                    sp.dma_start(v_tail[rows, :, :, j, :], vt_scratch[b].rearrange("r s (g j d) -> r s g j d", g=G, j=4)[:, :, :, j, :]).then_inc(kv_loaded, 16)
                sp.dma_start(v_main[:, :, :], v_scratch[b]).then_inc(kv_loaded, 16)

            def store_out(i, t):
                sp.wait_ge(out_ready, i * TT + t + 1)
                sp.dma_start(out_tiles[i, t], x1[:, t, :]).then_inc(out_stored[t], 16)

            sp.wait_ge(ctx_transposed, 2 * B)
            for t in range(3):
                load_xa(0, t)
            sp.wait_ge(kv_stored, 48 * B)
            load_kv(0)
            sp.wait_ge(xT_done, 1)
            load_xa(0, 3)

            def step(i, ffn, pre):
                if pre:
                    sp.wait_ge(xT_done, (i + 1) * TT)
                    load_xa(i + 1, 0)
                    later(sp, xr_mixed, i * C)
                    load_xa(i + 1, 1)
                    load_xa(i + 1, 2)
                for t in range(TT):
                    if t == TT - 1 and pre:
                        sp.wait_ge(xT_done, (i + 1) * TT + 1)
                        load_xa(i + 1, 3)
                    if ffn:
                        store_out(i - 1, t)
                    if t == TT - 1 and pre:
                        load_kv(i + 1)
                    load_x1(i, t)

            step(0, False, True)
            with sp.Fori(1, BLOCKS - 1) as i:
                step(i, True, True)
            step(BLOCKS - 1, True, False)
            for t in range(TT):
                store_out(BLOCKS - 1, t)
            for t in range(TT):
                sp.wait_ge(out_stored[t], 16 * BLOCKS)

        @block.gpsimd
        def _(pool):
            done = [0]

            def link(ins):
                done[0] += 1
                ins.then_inc(chain["pool"], 1)
                pool.wait_ge(chain["pool"], done[0])

            link(nc.gpsimd.memset(ident[:, :], 0.0))
            link(nc.gpsimd.affine_select(out=ident[:, :], in_=ident[:, :], compare_op=ALU.not_equal, fill=1.0,
                                         base=0, pattern=[[-1, P]], channel_multiplier=1))
            heads = th[:, :].rearrange("p (h s) -> p h s", h=H)
            link(nc.gpsimd.memset(heads, 0.0))
            link(nc.gpsimd.affine_select(out=heads, in_=heads, compare_op=ALU.not_equal, fill=-1.0,
                                         base=0, pattern=[[-1, H], [0, TAIL]], channel_multiplier=1))
            link(nc.gpsimd.memset(ones_main[:, :], 1.0))
            link(nc.gpsimd.memset(ones_tail[:, :, :], 1.0))
            link(nc.gpsimd.affine_select(out=ones_tail[:, :, :], in_=ones_tail[:, :, :], compare_op=ALU.is_ge, fill=0.0,
                                         base=-OVER, pattern=[[-DH, 4], [0, DH]], channel_multiplier=1))
            link(nc.gpsimd.affine_select(out=ones_tail[:, :, :], in_=ones_tail[:, :, :], compare_op=ALU.is_ge, fill=0.0,
                                         base=DH - 1, pattern=[[DH, 4], [0, DH]], channel_multiplier=-1))
            link(nc.gpsimd.memset(mask[:, :], 1.0))
            link(nc.gpsimd.affine_select(out=mask[:, :], in_=mask[:, :], compare_op=ALU.is_ge, fill=0.0,
                                         base=-(P - TAIL + OVER), pattern=[[0, 1]], channel_multiplier=1))
            link(nc.gpsimd.memset(minus_half[:, :], -0.5))
            link(nc.gpsimd.memset(eps[:, :], EPS))
            link(nc.gpsimd.memset(flag[:, :], 1.0))
            link(nc.gpsimd.memset(flag[:, 0:BLOCKS:PER_BATCH], 0.0))
            link(nc.gpsimd.memset(carry[:, :], 0.0))
            link(nc.gpsimd.memset(mm[:, :, :], 0.0))
            link(nc.gpsimd.memset(k_pad[:].bitcast(F32), 0.0))
            link(nc.gpsimd.memset(k_tail[:].bitcast(F32), 0.0))
            nc.gpsimd.memset(v_tail[:, :, :, :, :], 0.0).then_inc(consts_ready, 1)

            def norm(which, i, t):
                n = i * TT + t + 1
                pool.wait_ge(mean_ready[which], n)
                nc.gpsimd.tensor_tensor(ve[:, which, t:t + 1], mv[:, which, t, 1:2], eps[:, :], ALU.add).then_inc(var_eps_ready[which], 1)
                pool.wait_ge(var_eps_ready[which], n)
                nc.gpsimd.tensor_tensor(rstd[:, which, t:t + 1], ve[:, which, t:t + 1], minus_half[:, :], ALU.pow).then_inc(rstd_ready[which], 1)
                pool.wait_ge(rstd_ready[which], n)
                nc.gpsimd.tensor_tensor(nb[:, which, t:t + 1], nm[:, which, t:t + 1], rstd[:, which, t:t + 1], ALU.mult).then_inc(norm_ready[which], 1)

            def difference(i, c):
                if c == 0:
                    pool.wait_ge(x2_ready, i * TT + TT)
                    pool.wait_ge(x2_first, i + 1)
                    later(pool, out_ready, i * TT)
                if c == 3:
                    pool.wait_ge(p_lo, (i + 1) * SCORE_UNITS)
                nc.gpsimd.tensor_tensor(diff[c], x2[:, c, 1:N + 1], x2[:, c, 0:N], ALU.subtract).then_inc(diff_ready, 1)

            def xr_low(i, c):
                pool.wait_ge(xr_hi, i * C + c + 1)
                nc.gpsimd.tensor_tensor(buf2[:, LO, c, :], mixed[c % 2], buf2[:, HI, c, :].bitcast(F32), ALU.subtract).then_inc(xr_lo, 1)

            def q_low(i, g):
                pool.wait_ge(q_copied, i * G + g + 1)
                nc.gpsimd.tensor_tensor(buf4[:, LO, g, :], tmp[:, 0, :], buf4[:, HI, g, :].bitcast(F32), ALU.subtract).then_inc(q_lo, 1)

            def k2_low(i, c):
                pool.wait_ge(k2_hi, i * C + c + 1)
                nc.gpsimd.tensor_tensor(buf1[:, LO, c, :], k2[c % 2], buf1[:, HI, c, :].bitcast(F32), ALU.subtract).then_inc(k2_lo, 1)

            def attn_low(i, g):
                pool.wait_ge(attn_hi, i * G + g + 1)
                nc.gpsimd.tensor_tensor(buf3[:, LO, g, :], tmp[:, 0, :], buf3[:, HI, g, :].bitcast(F32), ALU.subtract).then_inc(attn_lo, 1)

            for t in range(TT):
                norm(0, 0, t)
            for g in range(G):
                q_low(0, g)

            def step(i, ffn, pre):
                if ffn:
                    for c in range(C):
                        xr_low(i - 1, c)
                    for c in range(C):
                        k2_low(i - 1, c)
                for g in range(1, G):
                    attn_low(i, g - 1)
                    if pre:
                        norm(0, i + 1, g - 1)
                attn_low(i, G - 1)
                if pre:
                    norm(0, i + 1, 3)
                for t in range(TT):
                    norm(1, i, t)
                if pre:
                    q_low(i + 1, 0)
                    q_low(i + 1, 1)
                for c in range(C):
                    difference(i, c)
                    if c >= 2 and pre:
                        q_low(i + 1, c)

            step(0, False, True)
            with pool.Fori(1, BLOCKS - 1) as i:
                step(i, True, True)
            step(BLOCKS - 1, True, False)
            for c in range(C):
                xr_low(BLOCKS - 1, c)
            for c in range(C):
                k2_low(BLOCKS - 1, c)

        @block.scalar
        def _(act):
            act.wait_ge(small_loaded, 64)
            nc.scalar.activation(gate_tanh[:, 0:2], gate[:, 0:2], ACT.Tanh).then_inc(gates_ready, 1)

            def high(dst, src, done):
                nc.scalar.activation(dst, src, ACT.Copy).then_inc(done, 1)

            for n, (_, _, wT) in enumerate(weights):
                for c in range(C):
                    u = n * C + c
                    act.wait_ge(w_transposed, u + 1)
                    high(wT[:, HI, c, :], g_bank[u % 3][:, :], w_hi)
            def kv_high(b):
                for m in range(2):
                    act.wait_ge(ctx_transposed, 2 * b + m + 1)
                    later(act, kv_done, b * (G + 2))
                    high(buf3[:, HI, :, P * m:P * m + P], g_bank[m][:, :].rearrange("p (c n) -> p c n", c=C), ctx_hi)
                for g in range(G):
                    act.wait_ge(kv_done, b * (G + 2) + g + 1)
                    later(act, kv_stored, 48 * b)
                    high(buf4[:, HI, g, 0:2 * P], s_bank[g % 3][:, 0:2 * P], kv_hi)
                act.wait_ge(kv_done, b * (G + 2) + G + 1)
                high(tmp[:, 0, 0:D // 2].bitcast(F16), s_bank[1][:, :], kv_hi)
                act.wait_ge(kv_done, b * (G + 2) + G + 2)
                nc.scalar.activation(tmp[P - TAIL:P, 1, 0:D // 2].bitcast(F16), s_bank[2][P - TAIL:P, :], ACT.Copy,
                                     scale=mask[P - TAIL:P, :]).then_inc(kv_hi, 1)

            kv_high(0)
            with act.Fori(1, B) as b:
                kv_high(b)

            def norm1(i, t):
                act.wait_ge(norm_ready[0], i * TT + t + 1)
                nc.scalar.activation(xa[:, t % 3, :], xa[:, t % 3, :], ACT.Identity, bias=nb[:, 0, t:t + 1],
                                     scale=rstd[:, 0, t:t + 1]).then_inc(xn1_ready, 1)

            def norm2(i, t, pre):
                if t >= 2:
                    act.wait_ge(x2_done, i * TT + t - 1)
                elif pre:
                    act.wait_ge(xT_done, (i + 1) * TT + t + 2)
                act.wait_ge(norm_ready[1], i * TT + t + 1)
                nc.scalar.activation(xa[:, 1 + t % 2, :], x1[:, t, :], ACT.Identity, bias=nb[:, 1, t:t + 1],
                                     scale=rstd[:, 1, t:t + 1]).then_inc(xn2_ready, 1)

            def xT_high(i, t):
                act.wait_ge(xT_done, i * TT + t + 1)
                later(act, v_done, (i - 1) * TT)
                high(buf1[:, HI, :, P * t:P * t + P], g_bank[XT_BANK[t]][:, :].rearrange("p (c n) -> p c n", c=C), xT_hi)

            def q_high(i, g):
                act.wait_ge(q_done, i * G + g + 1)
                high(buf4[:, HI, g, :], g_bank[Q_BANK[g]][:, :], q_hi)
                if g:
                    act.wait_ge(q_lo, i * G + g)
                else:
                    later(act, attn_lo, i * G)
                high(tmp[:, 0, :], g_bank[Q_BANK[g]][:, :], q_copied)

            def k_square(i, c, pre):
                act.wait_ge(k_done, i * C + c + 1)
                if c >= 2:
                    act.wait_ge(k2_lo, i * C + c - 1)
                elif c == 1:
                    act.wait_ge(xr_mixed, i * C + 1)
                elif pre:
                    act.wait_ge(q_lo, (i + 2) * G)
                nc.scalar.activation(k2[c % 2], g_bank[K_BANK[c]][:, :], ACT.Relu).then_inc(relu_ready, 1)
                act.wait_ge(relu_ready, i * C + c + 1)
                nc.scalar.activation(k2[c % 2], k2[c % 2], ACT.Square).then_inc(k2_ready, 1)
                act.wait_ge(k2_ready, i * C + c + 1)
                high(buf1[:, HI, c, :], k2[c % 2], k2_hi)

            def exps(i, g, n):
                u = i * 5 * G + 5 * g + n
                bank = score_bank[5 * g + n]
                act.wait_ge(scores_done, u + 1)
                if n == 0:
                    if g == 0:
                        later(act, xk_lo, i * C)
                        later(act, xr_lo, i * C)
                    later(act, av_done, i * G + g)
                nc.scalar.activation(pq[:, n, HI, :], bank[:, :], ACT.Exp, scale=SCALE).then_inc(p_hi, 1)
                m = 5 * g + n
                if m == 1:
                    later(act, xr_mixed, i * C)
                if m >= 2:
                    act.wait_ge(p_lo, u - 1)
                nc.scalar.activation(p32[m % 2], bank[:, :], ACT.Exp, scale=SCALE).then_inc(p_full, 1)

            def tanh_r(i, t):
                act.wait_ge(r_done, i * TT + t + 1)
                if t:
                    act.wait_ge(out_ready, i * TT + t)
                else:
                    act.wait_ge(k2_lo, (i + 1) * C)
                nc.scalar.activation(th[:, :], g_bank[R_BANK[t]][:, :], ACT.Tanh, scale=0.5).then_inc(th_ready, 1)

            def attn_high(i, g):
                act.wait_ge(attn32_ready, i * G + g + 1)
                high(buf3[:, HI, g, :], tmp[:, 0, :], attn_hi)

            def x2_copy(i, t):
                act.wait_ge(x2_done, i * TT + t + 1)
                act.wait_ge(p_lo, (i + 1) * 5 * G)
                act.wait_ge(av_done, (i + 1) * G)
                nc.scalar.activation(x2[:, :, 1 + P * t:1 + P * t + P],
                                     x2_bank[t][:, :].rearrange("p (c n) -> p c n", c=C), ACT.Copy).then_inc(x2_ready, 1)

            def mix_high(i, dst, c, mixed_ready, hi_ready):
                act.wait_ge(mixed_ready, i * C + c + 1)
                high(dst[:, HI, c, :], mixed[c % 2], hi_ready)

            def mT_copy(i):
                act.wait_ge(mT_done, i + 1)
                high(mT[:, :], mT_bank[:, :], mT_ready)

            act.wait_ge(kv_stored, 48 * B)
            for t in range(3):
                norm1(0, t)
            for t in range(3):
                xT_high(0, t)
            norm1(0, 3)
            xT_high(0, 3)
            for g in range(G):
                q_high(0, g)
            mT_copy(0)

            def step(i, ffn, pre):
                if ffn:
                    k_square(i - 1, 0, True)
                exps(i, 0, 0)
                exps(i, 0, 1)
                if ffn:
                    k_square(i - 1, 1, True)
                exps(i, 0, 2)
                if ffn:
                    k_square(i - 1, 2, True)
                exps(i, 0, 3)
                exps(i, 0, 4)
                if ffn:
                    k_square(i - 1, 3, True)
                for g in range(1, G):
                    exps(i, g, 0)
                    exps(i, g, 1)
                    exps(i, g, 2)
                    if ffn:
                        tanh_r(i - 1, g - 1)
                    exps(i, g, 3)
                    exps(i, g, 4)
                    attn_high(i, g - 1)
                    if g >= 2 and pre:
                        norm1(i + 1, g - 2)
                if pre:
                    norm1(i + 1, 2)
                if ffn:
                    tanh_r(i - 1, TT - 1)
                attn_high(i, G - 1)
                if pre:
                    for t in range(3):
                        xT_high(i + 1, t)
                    norm1(i + 1, 3)
                norm2(i, 0, pre)
                if pre:
                    xT_high(i + 1, 3)
                norm2(i, 1, pre)
                x2_copy(i, 0)
                norm2(i, 2, pre)
                x2_copy(i, 1)
                if pre:
                    q_high(i + 1, 0)
                norm2(i, 3, pre)
                x2_copy(i, 2)
                if pre:
                    q_high(i + 1, 1)
                x2_copy(i, 3)
                if pre:
                    q_high(i + 1, 2)
                    q_high(i + 1, 3)
                mix_high(i, buf3, 0, xk_mixed, xk_hi)
                mix_high(i, buf3, 1, xk_mixed, xk_hi)
                if pre:
                    mT_copy(i + 1)
                mix_high(i, buf3, 2, xk_mixed, xk_hi)
                mix_high(i, buf3, 3, xk_mixed, xk_hi)
                for c in range(C):
                    mix_high(i, buf2, c, xr_mixed, xr_hi)

            step(0, False, True)
            with act.Fori(1, BLOCKS - 1) as i:
                step(i, True, True)
            step(BLOCKS - 1, True, False)
            for c in range(C):
                k_square(BLOCKS - 1, c, False)
            for t in range(TT):
                tanh_r(BLOCKS - 1, t)

        @block.vector
        def _(dve):
            def low(dst, src, hi, done):
                nc.vector.tensor_tensor(dst, src, hi.bitcast(F32), ALU.subtract).then_inc(done, 1)

            dve.wait_ge(consts_ready, 1)
            nc.vector.tensor_copy(negsel[:, :, :].rearrange("p h s -> p (h s)"), th[:, :]).then_inc(dve_small, 1)
            dve.wait_ge(gates_ready, 1)
            nc.vector.tensor_scalar(gate[:, 2:3], gate_tanh[:, 0:1], 1.0, None, ALU.mult).then_inc(dve_small, 1)
            nc.vector.tensor_scalar(gate[:, 3:4], gate_tanh[:, 1:2], 0.5, None, ALU.mult).then_inc(dve_small, 1)
            dve.wait_ge(dve_small, 3)
            for n, (_, _, wT) in enumerate(weights):
                for c in range(C):
                    u = n * C + c
                    dve.wait_ge(w_hi, u + 1)
                    low(wT[:, LO, c, :], g_bank[u % 3][:, :], wT[:, HI, c, :], w_lo)
            def kv_low(b):
                for m in range(2):
                    cols = slice(P * m, P * m + P)
                    dve.wait_ge(ctx_hi, 2 * b + m + 1)
                    low(buf3[:, LO, :, cols], g_bank[m][:, :].rearrange("p (c n) -> p c n", c=C), buf3[:, HI, :, cols], ctx_lo)
                for g in range(G):
                    dve.wait_ge(kv_hi, b * (G + 2) + g + 1)
                    low(buf4[:, LO, g, 0:2 * P], s_bank[g % 3][:, 0:2 * P], buf4[:, HI, g, 0:2 * P], kv_lo)
                dve.wait_ge(kv_hi, b * (G + 2) + G + 1)
                nc.vector.tensor_tensor(tmp[:, 0, D // 2:D].bitcast(F16), s_bank[1][:, :], tmp[:, 0, 0:D // 2].bitcast(F16),
                                        ALU.subtract).then_inc(kv_lo, 1)
                dve.wait_ge(kv_hi, b * (G + 2) + G + 2)
                tail = slice(P - TAIL, P)
                nc.vector.scalar_tensor_tensor(tmp[tail, 1, D // 2:D].bitcast(F16), s_bank[2][tail, :], mask[tail, :],
                                               tmp[tail, 1, 0:D // 2].bitcast(F16), ALU.mult, ALU.subtract).then_inc(kv_lo, 1)

            kv_low(0)
            with dve.Fori(1, B) as b:
                kv_low(b)

            def moments(which, i, t, src):
                n = i * TT + t + 1
                nc.vector.bn_stats(stats[:, which, t, :], src).then_inc(bn_ready[which], 1)
                dve.wait_ge(bn_ready[which], n)
                nc.vector.tensor_tensor(nm[:, which, t:t + 1], stats[:, which, t, 1:2], stats[:, which, t, 4:5], ALU.add).then_inc(sum_ready[which], 1)
                nc.vector.bn_aggr(mv[:, which, t, :], stats[:, which, t, :]).then_inc(aggr_ready[which], 1)
                dve.wait_ge(aggr_ready[which], n)
                dve.wait_ge(sum_ready[which], n)
                nc.vector.tensor_scalar(nm[:, which, t:t + 1], nm[:, which, t:t + 1], -0.5, None, ALU.mult).then_inc(mean_ready[which], 1)

            def moments1(i, t):
                dve.wait_ge(xa_loaded[t], 16 * (i + 1))
                moments(0, i, t, xa[:, t % 3, :])

            def xT_low(i, t):
                dve.wait_ge(xT_hi, i * TT + t + 1)
                cols = slice(P * t, P * t + P)
                src = g_bank[XT_BANK[t]][:, :].rearrange("p (c n) -> p c n", c=C)
                nc.vector.tensor_tensor(buf1[:, LO, :, cols], src, buf1[:, HI, :, cols].bitcast(F32), ALU.subtract).then_inc(xT_lo, 1)

            def reduce_max(i, n):
                if n == 0:
                    later(dve, mT_done, i)
                dve.wait_ge(max_done, i * MAX_UNITS + n + 1)
                g, t = n // TT, n % TT
                if g < G:
                    nc.vector.reduce_max(mm[:, t, 4 * g:4 * g + 4], max_bank[n][:, :].rearrange("p (h s) -> p h s", h=4), AX.X).then_inc(reduced, 1)
                else:
                    nc.vector.reduce_max(mx[:, t, :], max_bank[n][:, :].rearrange("p (h s) -> p h s", h=H), AX.X).then_inc(reduced, 1)

            def whole_max(i):
                dve.wait_ge(reduced, (i + 1) * MAX_UNITS)
                nc.vector.tensor_tensor(mm[:, :, 0:H], mm[:, :, 0:H], mx[:, :, :], ALU.max).then_inc(mm_ready, 1)

            def p_low(i, g, n):
                dve.wait_ge(p_full, i * 5 * G + 5 * g + n + 1)
                nc.vector.tensor_tensor(pq[:, n, LO, :], p32[(5 * g + n) % 2], pq[:, n, HI, :], ALU.subtract).then_inc(p_lo, 1)

            def attend(i, g):
                dve.wait_ge(av_done, i * G + g + 1)
                if g:
                    dve.wait_ge(attn_lo, i * G + g)
                nc.vector.reciprocal(tmp[:, 0, :], d_bank[:, :]).then_inc(recip_ready, 1)
                dve.wait_ge(recip_ready, i * G + g + 1)
                nc.vector.tensor_tensor(tmp[:, 0, :], o_bank[:, :], tmp[:, 0, :], ALU.mult).then_inc(attn32_ready, 1)

            def output(i, t):
                dve.wait_ge(th_ready, i * TT + t + 1)
                dve.wait_ge(v_done, i * TT + t + 1)
                nc.vector.scalar_tensor_tensor(th[:, :], th[:, :], 1.0, g_bank[V_BANK[t]][:, :], ALU.add, ALU.mult).then_inc(u_ready, 1)
                dve.wait_ge(u_ready, i * TT + t + 1)
                nc.vector.scalar_tensor_tensor(x1[:, t, :], th[:, :], gate[:, 3:4], x1[:, t, :], ALU.mult, ALU.add).then_inc(out_ready, 1)

            def residual(i, t):
                dve.wait_ge(x1_loaded[t], 16 * (i + 1))
                dve.wait_ge(wo_done, i * TT + t + 1)
                nc.vector.scalar_tensor_tensor(x1[:, t, :], g_bank[WO_BANK[t]][:, :], gate[:, 2:3], x1[:, t, :], ALU.mult, ALU.add).then_inc(x1_ready, 1)
                dve.wait_ge(x1_ready, i * TT + t + 1)
                moments(1, i, t, x1[:, t, :])

            def first_column(i):
                dve.wait_ge(av_done, (i + 1) * G)
                dve.wait_ge(p_lo, (i + 1) * 5 * G)
                later(dve, carry_ready, i)
                nc.vector.tensor_scalar(x2[:, :, 0], carry[:, :], flag[:, bass.ds(i, 1)], None, ALU.mult).then_inc(x2_first, 1)

            def keep_carry(i):
                dve.wait_ge(x2_ready, (i + 1) * TT)
                dve.wait_ge(x2_first, i + 1)
                nc.vector.tensor_copy(carry[:, :], x2[:, :, N]).then_inc(carry_ready, 1)

            def mix(i, c, which, mixed_ready):
                nc.vector.scalar_tensor_tensor(mixed[c % 2], diff[c], mu[:, which, c:c + 1], x2[:, c, 0:N], ALU.mult, ALU.add).then_inc(mixed_ready, 1)

            def mix_k(i, c):
                dve.wait_ge(diff_ready, i * C + c + 1)
                if c >= 2:
                    dve.wait_ge(xk_lo, i * C + c - 1)
                    dve.wait_ge(xk_hi, i * C + c - 1)
                mix(i, c, 1, xk_mixed)

            def mix_r(i, c):
                if c >= 2:
                    dve.wait_ge(xr_lo, i * C + c - 1)
                else:
                    dve.wait_ge(xk_lo, i * C + c + 3)
                mix(i, c, 0, xr_mixed)

            def xk_low(i, c):
                dve.wait_ge(xk_hi, i * C + c + 1)
                low(buf3[:, LO, c, :], mixed[c % 2], buf3[:, HI, c, :], xk_lo)

            dve.wait_ge(kv_stored, 48 * B)
            dve.wait_ge(small_loaded, 64)
            for t in range(3):
                moments1(0, t)
            for t in range(3):
                xT_low(0, t)
            moments1(0, 3)
            xT_low(0, 3)
            for n in range(MAX_UNITS):
                reduce_max(0, n)
            whole_max(0)

            def step(i, ffn, pre):
                if ffn:
                    for c in range(C):
                        mix_r(i - 1, c)
                for n in range(5):
                    p_low(i, 0, n)
                if ffn:
                    dve.wait_ge(k2_lo, i * C)
                for g in range(1, G):
                    p_low(i, g, 0)
                    p_low(i, g, 1)
                    p_low(i, g, 2)
                    attend(i, g - 1)
                    p_low(i, g, 3)
                    p_low(i, g, 4)
                    if ffn:
                        output(i - 1, g - 1)
                    if pre:
                        moments1(i + 1, g - 1)
                attend(i, G - 1)
                if ffn:
                    output(i - 1, TT - 1)
                first_column(i)
                if pre:
                    for t in range(3):
                        xT_low(i + 1, t)
                    moments1(i + 1, 3)
                for t in range(TT):
                    if t == TT - 1 and pre:
                        xT_low(i + 1, 3)
                    residual(i, t)
                if pre:
                    for n in range(3 * TT):
                        reduce_max(i + 1, n)
                keep_carry(i)
                parts = ((mix_k, 0), (mix_k, 1), (xk_low, 0), (mix_k, 2), (xk_low, 1), (mix_k, 3), (xk_low, 2), (xk_low, 3))
                for n, (part, c) in enumerate(parts):
                    if n == 3 and pre:
                        for m in range(3 * TT + 3, MAX_UNITS):
                            reduce_max(i + 1, m)
                        whole_max(i + 1)
                    part(i, c)
                    if n < 3 and pre:
                        reduce_max(i + 1, 3 * TT + n)

            step(0, False, True)
            with dve.Fori(1, BLOCKS - 1) as i:
                step(i, True, True)
            step(BLOCKS - 1, True, False)
            for c in range(C):
                mix_r(BLOCKS - 1, c)
            for t in range(TT):
                output(BLOCKS - 1, t)

        @block.tensor
        def _(pe):
            def product(dst, stationary, moving, chunks, before=None):
                for c in range(chunks):
                    if before:
                        before(c)
                    for n, (s, m) in enumerate(PRODUCTS):
                        ins = nc.tensor.matmul(dst, stationary(s, c), moving(m, c), start=(c, n) == (0, 0),
                                               stop=(c, n) == (chunks - 1, len(PRODUCTS) - 1))
                return ins

            def transposed(dst, tiles):
                for n, tile in enumerate(tiles):
                    ins = nc.tensor.transpose(dst[:, P * n:P * n + P], tile, ident[:, :])
                return ins

            def cols(n):
                return slice(P * n, P * n + P)

            pe.wait_ge(consts_ready, 1)
            for n in range(len(weights)):
                pe.wait_ge(nat_loaded[n % 2], 16 * (n // 2 + 1))
                for c in range(C):
                    u = n * C + c
                    if u >= 3:
                        pe.wait_ge(w_lo, u - 2)
                    transposed(g_bank[u % 3], [nat[n % 2][:, o, cols(c)] for o in range(C)]).then_inc(w_transposed, 1)
            pe.wait_ge(w_lo, C * len(weights))
            def keys_values(b):
                pe.wait_ge(ctx_loaded, 32 * b + 32)
                later(pe, ctx_lo, 2 * b)
                for m in range(2):
                    transposed(g_bank[m], [xa[:, m, cols(c)] for c in range(C)]).then_inc(ctx_transposed, 1)
                pe.wait_ge(ctx_lo, 2 * b + 2)
                later(pe, kv_lo, (G + 2) * b)
                for g in range(G):
                    if g == 3:
                        pe.wait_ge(kv_lo, (G + 2) * b + 1)
                    product(s_bank[g % 3][:, 0:2 * P], lambda s, c: buf1[:, s, c, cols(g)], lambda m, c: buf3[:, m, c, 0:2 * P],
                            C).then_inc(kv_done, 1)
                for n in range(2):
                    pe.wait_ge(kv_lo, (G + 2) * b + 2 + n)
                    product(s_bank[1 + n][:, :], lambda s, c: buf3[:, s, c, cols(n)], lambda m, c: buf2[:, m, c, :],
                            C).then_inc(kv_done, 1)

            keys_values(0)
            with pe.Fori(1, B) as b:
                keys_values(b)

            def xT(i, t):
                pe.wait_ge(xn1_ready, i * TT + t + 1)
                transposed(g_bank[XT_BANK[t]], [xa[:, t % 3, cols(c)] for c in range(C)]).then_inc(xT_done, 1)

            def maximum(i, n):
                g, t = n // TT, n % TT
                if n == 0:
                    pe.wait_ge(kv_loaded, 16 * KV_LOADS * (i + 1))
                if g < G and t == 0:
                    pe.wait_ge(q_hi, i * G + g + 1)
                if n >= 3:
                    pe.wait_ge(reduced, i * MAX_UNITS + n - 2)
                else:
                    later(pe, p_full, i * SCORE_UNITS)
                bank = max_bank[n]
                if g < G:
                    ins = nc.tensor.matmul(bank[:, :], buf4[:, HI, g, cols(t)], k_pad[:, HI, g, :, :].rearrange("p j s -> p (j s)"),
                                           start=True, stop=True)
                else:
                    for e in range(G):
                        ins = nc.tensor.matmul(bank[:, cols(e)], buf4[:, HI, e, cols(t)],
                                               k_tail[:, HI, e, :, :].rearrange("p j s -> p (j s)"), start=True, stop=True)
                ins.then_inc(max_done, 1)

            def query(i, g):
                def before(c):
                    n = TT * (g - 1) + c - 1
                    if n >= 0:
                        maximum(i, n)

                if g == 0:
                    pe.wait_ge(xT_lo, (i + 1) * TT)
                product(g_bank[Q_BANK[g]][:, :], lambda s, c: WqT[:, s, c, cols(g)], lambda m, c: buf1[:, m, c, :], C,
                        before).then_inc(q_done, 1)

            def maxima_left(i):
                for n in range(TT * (G - 1) - 1, MAX_UNITS):
                    maximum(i, n)

            def maxima_transposed(i):
                pe.wait_ge(mm_ready, i + 1)
                later(pe, x2_ready, i * TT - 1)
                transposed(mT_bank, [mm[:, t, :] for t in range(TT)]).then_inc(mT_done, 1)

            def score(i, g, n):
                for k, (s, q) in enumerate(PRODUCTS):
                    keys = k_pad[:, s, g, n, :] if n < 4 else k_tail[:, s, g, :, :].rearrange("p j s -> p (j s)")
                    nc.tensor.matmul(score_bank[5 * g + n][:, :], keys, buf4[:, q, g, :], start=k == 0, stop=False)

            def less_maximum(g, n):
                if n < 4:
                    shift = negsel[:, 4 * g + n, 0:1].to_broadcast([P, P])
                else:
                    shift = negsel[:, 4 * g:4 * g + 4, :].rearrange("p h s -> p (h s)")
                nc.tensor.matmul(score_bank[5 * g + n][:, :], shift, mT[:, :], start=False, stop=True).then_inc(scores_done, 1)

            def first_scores(i):
                pe.wait_ge(q_lo, (i + 1) * G)
                for n in range(3):
                    if n == 2:
                        maxima_transposed(i)
                    pe.wait_ge(reduced, (i + 1) * MAX_UNITS - 2 + n)
                    score(i, 0, n)
                pe.wait_ge(mT_ready, i + 1)
                for n in range(3):
                    less_maximum(0, n)

            def scores(i, g, units):
                for n in units:
                    pe.wait_ge(p_full, i * SCORE_UNITS + 5 * g + n - 2)
                    score(i, g, n)
                    less_maximum(g, n)

            def values(i, g):
                pe.wait_ge(p_lo, i * SCORE_UNITS + 5 * g + 5)
                later(pe, attn32_ready, i * G + g)
                if g == 0:
                    later(pe, x2_ready, i * TT)
                for n in range(2):
                    for k, (s, q) in enumerate(PRODUCTS):
                        for j in range(4):
                            v = v_main[:, s, DH * (4 * g + j):DH * (4 * g + j + 1)] if n == 0 else v_tail[:, s, g, j, :]
                            nc.tensor.matmul(o_bank[DH * j:DH * j + DH, :], v, pq[:, 4 if n else j, q, :],
                                             start=(n, k) == (0, 0), stop=(n, k) == (1, 2))
                for n in range(2):
                    for q in (HI, LO):
                        for j in range(4):
                            one = ones_main[:, :] if n == 0 else ones_tail[:, j, :]
                            ins = nc.tensor.matmul(d_bank[DH * j:DH * j + DH, :], one, pq[:, 4 if n else j, q, :],
                                                   start=(n, q) == (0, HI), stop=(n, q) == (1, LO))
                ins.then_inc(av_done, 1)

            def project(i, t):
                def whole(c):
                    if t == 0:
                        pe.wait_ge(attn_lo, i * G + c + 1)

                product(g_bank[WO_BANK[t]][:, :], lambda s, c: buf3[:, s, c, cols(t)], lambda m, c: WoT[:, m, c, :], C, whole).then_inc(wo_done, 1)

            def x2_transposed(i, t):
                pe.wait_ge(xn2_ready, i * TT + t + 1)
                if t < 2:
                    pe.wait_ge(attn32_ready, (i + 1) * G)
                else:
                    pe.wait_ge(x2_ready, i * TT + t - 1)
                transposed(x2_bank[t], [xa[:, 1 + t % 2, cols(c)] for c in range(C)]).then_inc(x2_done, 1)

            def ffn_k(i, c, queries=True):
                if c < 3:
                    if queries:
                        pe.wait_ge(q_copied, (i + 1) * G + c + 2)
                else:
                    pe.wait_ge(relu_ready, i * C + 1)

                def whole(e):
                    if c == 0:
                        pe.wait_ge(xk_lo, i * C + e + 1)

                product(g_bank[K_BANK[c]][:, :], lambda s, e: WkT2[:, s, e, cols(c)], lambda m, e: buf3[:, m, e, :], C, whole).then_inc(k_done, 1)

            def ffn_r(i, t):
                if t == 0:
                    pe.wait_ge(xr_lo, (i + 1) * C)
                pe.wait_ge(*((relu_ready, i * C + 2), (relu_ready, i * C + 4), (u_ready, i * TT + 1), (u_ready, i * TT + 2))[t])
                product(g_bank[R_BANK[t]][:, :], lambda s, c: buf2[:, s, c, cols(t)], lambda m, c: WrT[:, m, c, :], C).then_inc(r_done, 1)

            def ffn_v(i, t):
                if t == 0:
                    pe.wait_ge(k2_lo, (i + 1) * C)
                pe.wait_ge(*((relu_ready, i * C + 3), (th_ready, i * TT + 1), (th_ready, i * TT + 2), (th_ready, i * TT + 3))[t])
                product(g_bank[V_BANK[t]][:, :], lambda s, c: buf1[:, s, c, cols(t)], lambda m, c: WvT2[:, m, c, :], C).then_inc(v_done, 1)

            pe.wait_ge(kv_lo, (G + 2) * B)
            pe.wait_ge(kv_stored, 48 * B)
            for t in range(TT):
                xT(0, t)
            for g in range(G):
                if g == 3:
                    pe.wait_ge(q_copied, 1)
                query(0, g)
            maxima_left(0)

            def step(i, ffn, pre):
                first_scores(i)
                if ffn:
                    for c in range(3):
                        ffn_k(i - 1, c)
                scores(i, 0, (3, 4))
                if ffn:
                    ffn_k(i - 1, 3)
                for g in range(1, G):
                    scores(i, g, (0, 1, 2))
                    values(i, g - 1)
                    if ffn:
                        ffn_r(i - 1, g - 1)
                    scores(i, g, (3, 4))
                    if ffn:
                        ffn_v(i - 1, g - 1)
                if ffn:
                    ffn_r(i - 1, TT - 1)
                values(i, G - 1)
                if ffn:
                    ffn_v(i - 1, TT - 1)
                if pre:
                    for t in range(3):
                        if ffn:
                            pe.wait_ge(*((u_ready, i * TT - 1), (th_ready, i * TT), (u_ready, i * TT))[t])
                        else:
                            pe.wait_ge(q_copied, G)
                        xT(i + 1, t)
                else:
                    pe.wait_ge(u_ready, i * TT)
                for t in range(TT):
                    if t < 3 and pre:
                        pe.wait_ge(xT_lo, (i + 1) * TT + t + 1)
                    if t == 3:
                        if pre:
                            pe.wait_ge(x1_ready, i * TT + 1)
                            xT(i + 1, 3)
                        pe.wait_ge(x1_ready, i * TT + 2)
                    project(i, t)
                x2_transposed(i, 0)
                x2_transposed(i, 1)
                for g in range(G):
                    if pre:
                        pe.wait_ge(*((x1_ready, i * TT + 3), (xT_lo, (i + 2) * TT), (x1_ready, i * TT + 4), (q_copied, (i + 1) * G + 1))[g])
                        query(i + 1, g)
                    if g < 2:
                        x2_transposed(i, 2 + g)
                if pre:
                    maxima_left(i + 1)

            step(0, False, True)
            with pe.Fori(1, BLOCKS - 1) as i:
                step(i, True, True)
            step(BLOCKS - 1, True, False)
            pe.wait_ge(x1_ready, BLOCKS * TT)
            for c in range(C):
                ffn_k(BLOCKS - 1, c, queries=False)
            for t in range(TT):
                ffn_r(BLOCKS - 1, t)
                ffn_v(BLOCKS - 1, t)


NAMES = ("x", "ctx_1024", "g_xattn", "g_ffn", "L0_xattn_Wq", "L0_xattn_Wk", "L0_xattn_Wv", "L0_xattn_Wo",
         "L0_ffn_W_r", "L0_ffn_W_k", "L0_ffn_W_v", "L0_ffn_mu_r", "L0_ffn_mu_k")


def kernel(**inputs):
    import numpy as np
    import concourse.bacc as bacc
    from concourse.bass_utils import run_bass_kernel_spmd

    nc = bacc.Bacc("TRN2", target_bir_lowering=False, num_devices=1)
    arrays, args = {}, []
    for name in NAMES:
        a = np.ascontiguousarray(inputs[name])
        arrays[f"in_{name}"] = a
        args.append(nc.dram_tensor(f"in_{name}", a.shape, mybir.dt.from_np(a.dtype), kind="ExternalInput").ap())
    out = nc.dram_tensor("out_0", arrays["in_x"].shape, F32, kind="ExternalOutput").ap()
    flamingo_block(nc, *args, out)
    return run_bass_kernel_spmd(nc, [arrays], core_ids=[0]).results[0]["out_0"]
```

```python
from contextlib import ExitStack

import concourse.bass as bass
from concourse import mybir

F32 = mybir.dt.float32
F32R = mybir.dt.float32r
F16 = mybir.dt.float16
ALU = mybir.AluOpType
ACT = mybir.ActivationFunctionType
AX = mybir.AxisListType

HI, LO = 0, 1
PRODUCTS = ((HI, HI), (HI, LO), (LO, HI))


def flamingo_block(nc, x, ctx_tokens, g_xattn, g_ffn, Wq, Wk, Wv, Wo, W_r, W_k, W_v, mu_r, mu_k, out):
    B, T, D = x.shape
    S = ctx_tokens.shape[1]
    H = 16
    DH = D // H
    P = 128
    C = D // P
    G = H // 4
    N = 512
    TT = N // P
    BLOCKS = B * T // N
    PER_BATCH = T // N
    TAIL = 32
    OVER = P + TAIL - S
    SCALE = float(DH) ** -0.5
    EPS = 1e-5
    assert D == C * P == 512 and DH == 32 and C == G == TT and P < S <= P + TAIL and T % N == 0

    x_tiles = x.rearrange("b (n t p) d -> (b n) t p d", t=TT, p=P)
    out_tiles = out.rearrange("b (n t p) d -> (b n) t p d", t=TT, p=P)

    k_scratch = nc.dram_tensor("k_scratch", [B, P, 2, G, 2 * P], F32, kind="Internal").ap()
    v_scratch = nc.dram_tensor("v_scratch", [B, P, 2, D], F16, kind="Internal").ap()
    vt_scratch = nc.dram_tensor("vt_scratch", [B, TAIL, 2, D], F16, kind="Internal").ap()

    with ExitStack() as ctx:
        def sb(name, shape, dt):
            return ctx.enter_context(nc.sbuf_tensor(name, shape, dt))

        def psum(name):
            return ctx.enter_context(nc.psum_tensor(name, [P, 512], F32))

        def sem(name):
            return ctx.enter_context(nc.semaphore(name))

        WqT, WoT, WrT, WkT2, WvT2 = (sb(n, [P, 2, C, D], F32R) for n in ("WqT", "WoT", "WrT", "WkT2", "WvT2"))
        buf1 = sb("buf1", [P, 2, C, N], F32R)
        buf2 = sb("buf2", [P, 2, C, N], F32R)
        buf3 = sb("buf3", [P, 2, C, N], F32R)
        buf4 = sb("buf4", [P, 2, C, N], F32R)
        k_pad = sb("k_pad", [P, 2, G, 4, P], F32R)
        k_tail = sb("k_tail", [P, 2, G, 4, TAIL], F32R)
        v_main = sb("v_main", [P, 2, D], F16)
        v_tail = sb("v_tail", [P, 2, G, 4, TAIL], F16)
        ones_main = sb("ones_main", [P, DH], F16)
        ones_tail = sb("ones_tail", [P, 4, DH], F16)
        xa = sb("xa", [P, 3, D], F32)
        x1 = sb("x1", [P, TT, D], F32)
        ring = sb("ring", [P, C * (N + 1) + 2 * N], F32)
        tmp = sb("tmp", [P, 2, N], F32)
        th = sb("th", [P, N], F32)
        mm = sb("mm", [P, TT, P], F32)
        mT = sb("mT", [P, N], F32R)
        mx = sb("mx", [P, TT, H], F32)
        ident = sb("ident", [P, P], F32)
        negsel = sb("negsel", [P, H, TAIL], F32R)
        mask = sb("mask", [P, 1], F32)
        minus_half = sb("minus_half", [P, 1], F32)
        flag = sb("flag", [P, BLOCKS], F32)
        carry = sb("carry", [P, C], F32)
        mu = sb("mu", [P, 2, C], F32)
        gate = sb("gate", [P, 4], F32)
        gate_tanh = sb("gate_tanh", [P, 2], F32)
        stats = sb("stats", [P, 2, TT, 6], F32)
        mv = sb("mv", [P, 2, TT, 2], F32)
        nm = sb("nm", [P, 2, TT], F32)
        ve = sb("ve", [P, 2, TT], F32)
        rstd = sb("rstd", [P, 2, TT], F32)
        nb = sb("nb", [P, 2, TT], F32)
        eps = sb("eps", [P, 1], F32)

        p32 = (ring[:, 0:N], tmp[:, 1, :])
        pq = ring[:, N:6 * N].bitcast(F16).rearrange("p (c s n) -> p c s n", c=5, s=2)
        X2W = N + 1
        x2 = ring[:, 0:C * X2W].rearrange("p (c n) -> p c n", c=C)
        k2 = (tmp[:, 0, :], th[:, :])
        diff = (th[:, :], xa[:, 1, :], xa[:, 2, :], tmp[:, 1, :])
        xk32 = (ring[:, C * X2W:C * X2W + N], ring[:, C * X2W + N:C * X2W + 2 * N], xa[:, 0, :], tmp[:, 0, :])

        s_bank = [psum(f"s_bank{n}") for n in range(3)]
        o_bank, d_bank = psum("o_bank"), psum("d_bank")
        g_bank = [psum(f"g_bank{n}") for n in range(3)]

        ident_ready, heads_ready, consts_ready = sem("ident_ready"), sem("heads_ready"), sem("consts_ready")
        chain = {n: sem(f"chain_{n}") for n in ("pool", "act")}
        small_loaded = sem("small_loaded")
        gates_ready = sem("gates_ready")
        nat_loaded = [sem(f"nat_loaded{n}") for n in range(8)]
        w_transposed = sem("w_transposed")
        w_hi = sem("w_hi")
        w_lo = sem("w_lo")
        ctx_loaded = sem("ctx_loaded")
        ctx_transposed = sem("ctx_transposed")
        ctx_hi = sem("ctx_hi")
        ctx_lo = sem("ctx_lo")
        kv_done = sem("kv_done")
        kv_hi = sem("kv_hi")
        kv_lo = sem("kv_lo")
        kv_stored = sem("kv_stored")
        kv_loaded = sem("kv_loaded")
        xa_loaded = [sem(f"xa_loaded{t}") for t in range(TT)]
        x1_loaded = [sem(f"x1_loaded{t}") for t in range(TT)]
        out_stored = [sem(f"out_stored{t}") for t in range(TT)]
        bn_ready, sum_ready, aggr_ready, mean_ready, var_eps_ready, rstd_ready, norm_ready = (
            [sem(f"{n}{which}") for which in (1, 2)]
            for n in ("bn_ready", "sum_ready", "aggr_ready", "mean_ready", "var_eps_ready", "rstd_ready", "norm_ready"))
        dve_small = sem("dve_small")
        xn1_ready = sem("xn1_ready")
        xn2_ready = sem("xn2_ready")
        xT_done, xT_hi, xT_lo = sem("xT_done"), sem("xT_hi"), sem("xT_lo")
        q_done, q_hi, q_copied, q_lo = sem("q_done"), sem("q_hi"), sem("q_copied"), sem("q_lo")
        max_done = sem("max_done")
        reduced = sem("reduced")
        mm_ready, mT_done, mT_ready = sem("mm_ready"), sem("mT_done"), sem("mT_ready")
        scores_done = sem("scores_done")
        p_hi, p_full, p_lo = sem("p_hi"), sem("p_full"), sem("p_lo")
        av_done = sem("av_done")
        recip_ready, attn32_ready = sem("recip_ready"), sem("attn32_ready")
        attn_hi, attn_lo = sem("attn_hi"), sem("attn_lo")
        wo_done, x1_ready = sem("wo_done"), sem("x1_ready")
        x2_done, x2_ready = sem("x2_done"), sem("x2_ready")
        x2_first, carry_ready = sem("x2_first"), sem("carry_ready")
        diff_ready = sem("diff_ready")
        xk_mixed, xk_hi = sem("xk_mixed"), sem("xk_hi")
        xr_mixed, xr_hi = sem("xr_mixed"), sem("xr_hi")
        xk_lo, xr_lo = ([sem(n + "_lo12"), sem(n + "_lo03")] for n in ("xk", "xr"))
        k_done, relu_ready, k2_ready, k2_hi, k2_lo = (sem(n) for n in ("k_done", "relu_ready", "k2_ready", "k2_hi", "k2_lo"))
        r_done, th_ready, v_done, u_ready, out_ready = (sem(n) for n in ("r_done", "th_ready", "v_done", "u_ready", "out_ready"))
        WO_BANK, Q_BANK = (0, 1, 2, 1), (2, 0, 1, 2)
        K_BANK, R_BANK, V_BANK = (0, 1, 2, 0), (1, 0, 2, 1), (2, 1, 0, 2)
        SCORE_UNITS, MAX_UNITS = G * 5, TT * G + TT
        score_bank = [s_bank[(m + 1) % 3] for m in range(SCORE_UNITS)]
        max_bank = [s_bank[(SCORE_UNITS + n) % 3] for n in range(MAX_UNITS)]
        xT_bank = s_bank + [g_bank[0]]
        x2_bank = [(o_bank, d_bank)[t % 2] for t in range(TT)]
        mT_bank = o_bank
        KV_LOADS = 13

        early = ((Wk, buf1), (Wv, buf2), (Wq, WqT))
        late = ((Wo, WoT), (W_k, WkT2), (W_r, WrT), (W_v, WvT2))
        weights = early + late
        EARLY_UNITS, ALL_UNITS = C * len(early), C * len(weights)
        ring_nat = ring[:, 0:C * D].rearrange("p (c n) -> p c n", c=C)

        def nat_place(u):
            return u % 8 if u < EARLY_UNITS else u % 4

        def nat(u):
            place = nat_place(u)
            return x1[:, place, :] if place < 4 else ring_nat[:, place - 4, :]

        def nat_loads(u):
            return sum(nat_place(v) == nat_place(u) for v in range(u + 1))

        ctx_nat = ring[:, C * D:C * D + 2 * D].rearrange("p (m n) -> p m n", m=2)
        ctx_bank = (o_bank, d_bank)

        def x_tile(t, first=False):
            return th[:, :] if first and t == 3 else xa[:, t % 3, :]

        block = ctx.enter_context(nc.Block())

        def wait_lo(eng, pair, i, c):
            later(eng, pair[c in (0, 3)], 2 * i + 1 + c // 2)

        def later(eng, semaphore, value):
            if not isinstance(value, int) or value > 0:
                eng.wait_ge(semaphore, value)

        @block.sync
        def _(sp):
            def load_weight(u):
                if u >= EARLY_UNITS:
                    sp.wait_ge(w_transposed, u - 3)
                elif u >= 8:
                    sp.wait_ge(w_transposed, u - 7)
                sp.dma_start(nat(u), weights[u // C][0][P * (u % C):P * (u % C) + P, :]).then_inc(nat_loaded[nat_place(u)], 16)

            def load_ctx(b):
                later(sp, ctx_transposed, b * 2)
                sp.dma_start(ctx_nat[:, 0, :], ctx_tokens[b, 0:P, :]).then_inc(ctx_loaded, 16)
                sp.dma_start(ctx_nat[:, 1, :], ctx_tokens[b, S - P:S, :]).then_inc(ctx_loaded, 16)

            def store_kv(b):
                sp.wait_ge(kv_lo, b * (G + 2) + G + 2)
                sp.wait_ge(kv_hi, b * (G + 2) + G + 2)
                sp.dma_start(k_scratch[b], buf4[:, :, :, 0:2 * P].bitcast(F32)).then_inc(kv_stored, 16)
                sp.dma_start(v_scratch[b], tmp[:, 0, :].bitcast(F16).rearrange("p (s n) -> p s n", s=2)).then_inc(kv_stored, 16)
                sp.dma_start(vt_scratch[b], tmp[P - TAIL:P, 1, :].bitcast(F16).rearrange("p (s n) -> p s n", s=2)).then_inc(kv_stored, 16)

            def load_xa(i, t, first=False):
                sp.dma_start(x_tile(t, first), x_tiles[i, t]).then_inc(xa_loaded[t], 16)

            def load_x1(i, t):
                later(sp, out_stored[t], 16 * i)
                sp.dma_start(x1[:, t, :], x_tiles[i, t]).then_inc(x1_loaded[t], 16)

            def load_kv(i):
                later(sp, av_done, i * G)
                b = i // PER_BATCH
                for j in range(4):
                    rows = slice(DH * j, DH * j + DH)
                    sp.dma_start(k_pad[rows, :, :, j, :].bitcast(F32), k_scratch[b, rows, :, :, 0:P]).then_inc(kv_loaded, 16)
                    sp.dma_start(k_tail[rows, :, :, j, :].bitcast(F32), k_scratch[b, rows, :, :, 2 * P - TAIL:2 * P]).then_inc(kv_loaded, 16)
                    sp.dma_start(v_tail[rows, :, :, j, :], vt_scratch[b].rearrange("r s (g j d) -> r s g j d", g=G, j=4)[:, :, :, j, :]).then_inc(kv_loaded, 16)
                sp.dma_start(v_main[:, :, :], v_scratch[b]).then_inc(kv_loaded, 16)

            def store_out(i, t):
                sp.wait_ge(out_ready, i * TT + t + 1)
                sp.dma_start(out_tiles[i, t], x1[:, t, :]).then_inc(out_stored[t], 16)

            for u in range(8):
                load_weight(u)
            load_ctx(0)
            for col, g in enumerate((g_xattn, g_ffn)):
                sp.dma_start(gate[:, col:col + 1], g.rearrange("(a n) -> a n", a=1).to_broadcast([P, 1])).then_inc(small_loaded, 16)
            for n, m in enumerate((mu_r, mu_k)):
                sp.dma_start(mu[:, n, :], m.rearrange("(c p) -> p c", p=P), allow_slow_non_contiguous=True).then_inc(small_loaded, 16)
            for t in range(3):
                load_xa(0, t)
            sp.wait_ge(dve_small, 1)
            load_xa(0, 3, True)
            for u in range(8, EARLY_UNITS + C):
                load_weight(u)
            load_ctx(1)
            store_kv(0)
            with sp.Fori(1, B - 1) as b:
                load_ctx(b + 1)
                store_kv(b)
            sp.wait_ge(consts_ready, 1)
            sp.wait_ge(kv_stored, 48 * (B - 1))
            load_kv(0)
            store_kv(B - 1)

            def step(i, ffn, pre):
                if pre:
                    sp.wait_ge(xT_done, (i + 1) * TT)
                    wait_lo(sp, xk_lo, i - 1, 2)
                    load_xa(i + 1, 0)
                    wait_lo(sp, xr_lo, i - 1, 2)
                    load_xa(i + 1, 1)
                    load_xa(i + 1, 2)
                if not ffn:
                    for u in range(EARLY_UNITS + C, ALL_UNITS):
                        load_weight(u)
                    sp.wait_ge(w_transposed, ALL_UNITS)
                for t in range(TT):
                    if t == TT - 1 and pre:
                        sp.wait_ge(xT_done, (i + 1) * TT + 1)
                        load_xa(i + 1, 3)
                    if ffn:
                        store_out(i - 1, t)
                    if t == TT - 1 and pre:
                        load_kv(i + 1)
                    load_x1(i, t)

            step(0, False, True)
            with sp.Fori(1, BLOCKS - 1) as i:
                step(i, True, True)
            step(BLOCKS - 1, True, False)
            for t in range(TT):
                store_out(BLOCKS - 1, t)
            for t in range(TT):
                sp.wait_ge(out_stored[t], 16 * BLOCKS)

        @block.gpsimd
        def _(pool):
            done = [0]

            def link(ins):
                done[0] += 1
                ins.then_inc(chain["pool"], 1)
                pool.wait_ge(chain["pool"], done[0])

            link(nc.gpsimd.memset(ident[:, :], 0.0))
            link(nc.gpsimd.affine_select(out=ident[:, :], in_=ident[:, :], compare_op=ALU.not_equal, fill=1.0,
                                         base=0, pattern=[[-1, P]], channel_multiplier=1))
            nc.gpsimd.memset(flag[:, :], 1.0).then_inc(ident_ready, 1)
            heads = th[:, :].rearrange("p (h s) -> p h s", h=H)
            link(nc.gpsimd.memset(heads, 0.0))
            link(nc.gpsimd.affine_select(out=heads, in_=heads, compare_op=ALU.not_equal, fill=-1.0,
                                         base=0, pattern=[[-1, H], [0, TAIL]], channel_multiplier=1))
            nc.gpsimd.memset(minus_half[:, :], -0.5).then_inc(heads_ready, 1)
            link(nc.gpsimd.memset(ones_main[:, :], 1.0))
            link(nc.gpsimd.memset(ones_tail[:, :, :], 1.0))
            link(nc.gpsimd.affine_select(out=ones_tail[:, :, :], in_=ones_tail[:, :, :], compare_op=ALU.is_ge, fill=0.0,
                                         base=-OVER, pattern=[[-DH, 4], [0, DH]], channel_multiplier=1))
            link(nc.gpsimd.affine_select(out=ones_tail[:, :, :], in_=ones_tail[:, :, :], compare_op=ALU.is_ge, fill=0.0,
                                         base=DH - 1, pattern=[[DH, 4], [0, DH]], channel_multiplier=-1))
            link(nc.gpsimd.memset(mask[:, :], 1.0))
            link(nc.gpsimd.affine_select(out=mask[:, :], in_=mask[:, :], compare_op=ALU.is_ge, fill=0.0,
                                         base=-(P - TAIL + OVER), pattern=[[0, 1]], channel_multiplier=1))
            pool.wait_ge(heads_ready, 1)
            link(nc.gpsimd.memset(eps[:, :], EPS))
            pool.wait_ge(ident_ready, 1)
            link(nc.gpsimd.memset(flag[:, 0:BLOCKS:PER_BATCH], 0.0))
            link(nc.gpsimd.memset(carry[:, :], 0.0))
            link(nc.gpsimd.memset(mm[:, :, :], 0.0))
            link(nc.gpsimd.memset(k_pad[:].bitcast(F32), 0.0))
            link(nc.gpsimd.memset(k_tail[:].bitcast(F32), 0.0))
            nc.gpsimd.memset(v_tail[:, :, :, :, :], 0.0).then_inc(consts_ready, 1)

            def norm(which, i, t):
                n = i * TT + t + 1
                pool.wait_ge(mean_ready[which], n)
                nc.gpsimd.tensor_tensor(ve[:, which, t:t + 1], mv[:, which, t, 1:2], eps[:, :], ALU.add).then_inc(var_eps_ready[which], 1)
                pool.wait_ge(var_eps_ready[which], n)
                nc.gpsimd.tensor_tensor(rstd[:, which, t:t + 1], ve[:, which, t:t + 1], minus_half[:, :], ALU.pow).then_inc(rstd_ready[which], 1)
                pool.wait_ge(rstd_ready[which], n)
                nc.gpsimd.tensor_tensor(nb[:, which, t:t + 1], nm[:, which, t:t + 1], rstd[:, which, t:t + 1], ALU.mult).then_inc(norm_ready[which], 1)

            def difference(i, c):
                if c == 0:
                    pool.wait_ge(x2_ready, i * TT + TT)
                    pool.wait_ge(x2_first, i + 1)
                    later(pool, out_ready, i * TT)
                if c == 3:
                    pool.wait_ge(p_lo, (i + 1) * SCORE_UNITS)
                nc.gpsimd.tensor_tensor(diff[c], x2[:, c, 1:N + 1], x2[:, c, 0:N], ALU.subtract).then_inc(diff_ready, 1)

            def mix_low(i, dst, c, src, hi_ready, lo_ready):
                pool.wait_ge(hi_ready, i * C + c + 1)
                nc.gpsimd.tensor_tensor(dst[:, LO, c, :], src[c], dst[:, HI, c, :].bitcast(F32), ALU.subtract).then_inc(lo_ready[0], 1)

            def q_low(i, g):
                pool.wait_ge(q_copied, i * G + g + 1)
                nc.gpsimd.tensor_tensor(buf4[:, LO, g, :], tmp[:, 0, :], buf4[:, HI, g, :].bitcast(F32), ALU.subtract).then_inc(q_lo, 1)

            def k2_low(i, c):
                pool.wait_ge(k2_hi, i * C + c + 1)
                nc.gpsimd.tensor_tensor(buf1[:, LO, c, :], k2[c % 2], buf1[:, HI, c, :].bitcast(F32), ALU.subtract).then_inc(k2_lo, 1)

            def attn_low(i, g):
                pool.wait_ge(attn_hi, i * G + g + 1)
                nc.gpsimd.tensor_tensor(buf3[:, LO, g, :], tmp[:, 0, :], buf3[:, HI, g, :].bitcast(F32), ALU.subtract).then_inc(attn_lo, 1)

            for t in range(TT):
                norm(0, 0, t)
            for g in range(G):
                q_low(0, g)

            def step(i, ffn, pre):
                if ffn:
                    for c in (1, 2):
                        mix_low(i - 1, buf2, c, diff, xr_hi, xr_lo)
                    for c in range(C):
                        k2_low(i - 1, c)
                for g in range(1, G):
                    attn_low(i, g - 1)
                    if pre:
                        norm(0, i + 1, g - 1)
                attn_low(i, G - 1)
                if pre:
                    norm(0, i + 1, 3)
                for t in range(TT):
                    norm(1, i, t)
                if pre:
                    q_low(i + 1, 0)
                    q_low(i + 1, 1)
                for c in range(C):
                    difference(i, c)
                    if c >= 2 and pre:
                        q_low(i + 1, c)
                for c in (1, 2):
                    mix_low(i, buf3, c, xk32, xk_hi, xk_lo)

            step(0, False, True)
            with pool.Fori(1, BLOCKS - 1) as i:
                step(i, True, True)
            step(BLOCKS - 1, True, False)
            for c in (1, 2):
                mix_low(BLOCKS - 1, buf2, c, diff, xr_hi, xr_lo)
            for c in range(C):
                k2_low(BLOCKS - 1, c)

        @block.scalar
        def _(act):
            act.wait_ge(small_loaded, 64)
            nc.scalar.activation(gate_tanh[:, 0:2], gate[:, 0:2], ACT.Tanh).then_inc(gates_ready, 1)

            def high(dst, src, done):
                nc.scalar.activation(dst, src, ACT.Copy).then_inc(done, 1)

            def weight_high(u):
                act.wait_ge(w_transposed, u + 1)
                high(weights[u // C][1][:, HI, :, P * (u % C):P * (u % C) + P], g_bank[u % 3][:, :].rearrange("p (c n) -> p c n", c=C), w_hi)

            for u in range(EARLY_UNITS):
                weight_high(u)
            def kv_high(b):
                for m in range(2):
                    act.wait_ge(ctx_transposed, 2 * b + m + 1)
                    later(act, kv_done, b * (G + 2))
                    high(buf3[:, HI, :, P * m:P * m + P], ctx_bank[m][:, :].rearrange("p (c n) -> p c n", c=C), ctx_hi)
                for g in range(G):
                    act.wait_ge(kv_done, b * (G + 2) + g + 1)
                    later(act, kv_stored, 48 * b)
                    high(buf4[:, HI, g, 0:2 * P], s_bank[g % 3][:, 0:2 * P], kv_hi)
                act.wait_ge(kv_done, b * (G + 2) + G + 1)
                high(tmp[:, 0, 0:D // 2].bitcast(F16), s_bank[1][:, :], kv_hi)
                act.wait_ge(kv_done, b * (G + 2) + G + 2)
                nc.scalar.activation(tmp[P - TAIL:P, 1, 0:D // 2].bitcast(F16), s_bank[2][P - TAIL:P, :], ACT.Copy,
                                     scale=mask[P - TAIL:P, :]).then_inc(kv_hi, 1)

            def norm1(i, t, first=False):
                act.wait_ge(norm_ready[0], i * TT + t + 1)
                nc.scalar.activation(x_tile(t, first), x_tile(t, first), ACT.Identity, bias=nb[:, 0, t:t + 1],
                                     scale=rstd[:, 0, t:t + 1]).then_inc(xn1_ready, 1)

            for t in range(TT):
                norm1(0, t, True)
            kv_high(0)
            with act.Fori(1, B) as b:
                kv_high(b)

            def norm2(i, t, pre):
                if t >= 2:
                    act.wait_ge(x2_done, i * TT + t - 1)
                elif pre:
                    act.wait_ge(xT_done, (i + 1) * TT + t + 2)
                act.wait_ge(norm_ready[1], i * TT + t + 1)
                nc.scalar.activation(xa[:, 1 + t % 2, :], x1[:, t, :], ACT.Identity, bias=nb[:, 1, t:t + 1],
                                     scale=rstd[:, 1, t:t + 1]).then_inc(xn2_ready, 1)

            def xT_high(i, t):
                act.wait_ge(xT_done, i * TT + t + 1)
                later(act, v_done, (i - 1) * TT)
                high(buf1[:, HI, :, P * t:P * t + P], xT_bank[t][:, :].rearrange("p (c n) -> p c n", c=C), xT_hi)

            def q_high(i, g):
                act.wait_ge(q_done, i * G + g + 1)
                high(buf4[:, HI, g, :], g_bank[Q_BANK[g]][:, :], q_hi)
                if g:
                    act.wait_ge(q_lo, i * G + g)
                else:
                    later(act, attn_lo, i * G)
                high(tmp[:, 0, :], g_bank[Q_BANK[g]][:, :], q_copied)

            def k_relu(i, c):
                act.wait_ge(k_done, i * C + c + 1)
                if c >= 2:
                    act.wait_ge(k2_lo, i * C + c - 1)
                elif c == 1:
                    wait_lo(act, xr_lo, i, 0)
                else:
                    wait_lo(act, xk_lo, i, 3)
                nc.scalar.activation(k2[c % 2], g_bank[K_BANK[c]][:, :], ACT.Relu).then_inc(relu_ready, 1)

            def k_square(i, c):
                act.wait_ge(relu_ready, i * C + c + 1)
                nc.scalar.activation(k2[c % 2], k2[c % 2], ACT.Square).then_inc(k2_ready, 1)

            def k2_high(i, c):
                act.wait_ge(k2_ready, i * C + c + 1)
                high(buf1[:, HI, c, :], k2[c % 2], k2_hi)

            def relu_squared(i, c):
                k_relu(i, c)
                k_square(i, c)
                k2_high(i, c)

            def exps(i, g, n):
                u = i * 5 * G + 5 * g + n
                bank = score_bank[5 * g + n]
                act.wait_ge(scores_done, u + 1)
                if n == 0:
                    if g == 0:
                        wait_lo(act, xk_lo, i - 1, 0)
                        wait_lo(act, xk_lo, i - 1, 1)
                        later(act, xr_mixed, i * C)
                    later(act, av_done, i * G + g)
                nc.scalar.activation(pq[:, n, HI, :], bank[:, :], ACT.Exp, scale=SCALE).then_inc(p_hi, 1)
                m = 5 * g + n
                if m == 1:
                    wait_lo(act, xr_lo, i - 1, 3)
                if m >= 2:
                    act.wait_ge(p_lo, u - 1)
                nc.scalar.activation(p32[m % 2], bank[:, :], ACT.Exp, scale=SCALE).then_inc(p_full, 1)

            def tanh_r(i, t):
                act.wait_ge(r_done, i * TT + t + 1)
                if t:
                    act.wait_ge(out_ready, i * TT + t)
                else:
                    act.wait_ge(k2_lo, (i + 1) * C)
                nc.scalar.activation(th[:, :], g_bank[R_BANK[t]][:, :], ACT.Tanh, scale=0.5).then_inc(th_ready, 1)

            def attn_high(i, g):
                act.wait_ge(attn32_ready, i * G + g + 1)
                high(buf3[:, HI, g, :], tmp[:, 0, :], attn_hi)

            def x2_copy(i, t):
                act.wait_ge(x2_done, i * TT + t + 1)
                act.wait_ge(p_lo, (i + 1) * 5 * G)
                act.wait_ge(av_done, (i + 1) * G)
                nc.scalar.activation(x2[:, :, 1 + P * t:1 + P * t + P],
                                     x2_bank[t][:, :].rearrange("p (c n) -> p c n", c=C), ACT.Copy).then_inc(x2_ready, 1)

            def mix_high(i, dst, c, src, mixed_ready, hi_ready):
                act.wait_ge(mixed_ready, i * C + c + 1)
                high(dst[:, HI, c, :], src[c], hi_ready)

            def mT_copy(i):
                act.wait_ge(mT_done, i + 1)
                high(mT[:, :], mT_bank[:, :], mT_ready)

            act.wait_ge(kv_done, B * (G + 2))
            for t in range(TT):
                xT_high(0, t)
            act.wait_ge(kv_stored, 48 * B)
            for g in range(G):
                q_high(0, g)
            mT_copy(0)

            def step(i, ffn, pre):
                if ffn:
                    for c in range(C):
                        mix_high(i - 1, buf2, c, diff, xr_mixed, xr_hi)
                exps(i, 0, 0)
                exps(i, 0, 1)
                if ffn:
                    relu_squared(i - 1, 0)
                exps(i, 0, 2)
                if ffn:
                    relu_squared(i - 1, 1)
                exps(i, 0, 3)
                exps(i, 0, 4)
                if ffn:
                    relu_squared(i - 1, 2)
                    relu_squared(i - 1, 3)
                else:
                    for u in range(EARLY_UNITS, EARLY_UNITS + C):
                        weight_high(u)
                for g in range(1, G):
                    exps(i, g, 0)
                    exps(i, g, 1)
                    exps(i, g, 2)
                    if ffn:
                        tanh_r(i - 1, g - 1)
                    exps(i, g, 3)
                    exps(i, g, 4)
                    attn_high(i, g - 1)
                    if not ffn:
                        for u in range(EARLY_UNITS + C * g, EARLY_UNITS + C * g + C):
                            weight_high(u)
                    if g >= 2 and pre:
                        norm1(i + 1, g - 2)
                if pre:
                    norm1(i + 1, 2)
                if ffn:
                    tanh_r(i - 1, TT - 1)
                attn_high(i, G - 1)
                if pre:
                    for t in range(3):
                        xT_high(i + 1, t)
                    norm1(i + 1, 3)
                norm2(i, 0, pre)
                if pre:
                    xT_high(i + 1, 3)
                norm2(i, 1, pre)
                x2_copy(i, 0)
                norm2(i, 2, pre)
                x2_copy(i, 1)
                if pre:
                    q_high(i + 1, 0)
                norm2(i, 3, pre)
                x2_copy(i, 2)
                if pre:
                    q_high(i + 1, 1)
                x2_copy(i, 3)
                if pre:
                    q_high(i + 1, 2)
                    q_high(i + 1, 3)
                if pre:
                    mT_copy(i + 1)
                for c in range(C):
                    mix_high(i, buf3, c, xk32, xk_mixed, xk_hi)

            step(0, False, True)
            with act.Fori(1, BLOCKS - 1) as i:
                step(i, True, True)
            step(BLOCKS - 1, True, False)
            for c in range(C):
                mix_high(BLOCKS - 1, buf2, c, diff, xr_mixed, xr_hi)
            for c in range(C):
                relu_squared(BLOCKS - 1, c)
            for t in range(TT):
                tanh_r(BLOCKS - 1, t)

        @block.vector
        def _(dve):
            def low(dst, src, hi, done):
                nc.vector.tensor_tensor(dst, src, hi.bitcast(F32), ALU.subtract).then_inc(done, 1)

            dve.wait_ge(heads_ready, 1)
            nc.vector.tensor_copy(negsel[:, :, :].rearrange("p h s -> p (h s)"), th[:, :]).then_inc(dve_small, 1)

            def weight_low(units):
                for u in units:
                    dve.wait_ge(w_hi, u + 1)
                    wT, cols = weights[u // C][1], slice(P * (u % C), P * (u % C) + P)
                    low(wT[:, LO, :, cols], g_bank[u % 3][:, :].rearrange("p (c n) -> p c n", c=C), wT[:, HI, :, cols], w_lo)

            def kv_low(b):
                for m in range(2):
                    cols = slice(P * m, P * m + P)
                    dve.wait_ge(ctx_hi, 2 * b + m + 1)
                    low(buf3[:, LO, :, cols], ctx_bank[m][:, :].rearrange("p (c n) -> p c n", c=C), buf3[:, HI, :, cols], ctx_lo)
                for g in range(G):
                    dve.wait_ge(kv_hi, b * (G + 2) + g + 1)
                    low(buf4[:, LO, g, 0:2 * P], s_bank[g % 3][:, 0:2 * P], buf4[:, HI, g, 0:2 * P], kv_lo)
                dve.wait_ge(kv_hi, b * (G + 2) + G + 1)
                nc.vector.tensor_tensor(tmp[:, 0, D // 2:D].bitcast(F16), s_bank[1][:, :], tmp[:, 0, 0:D // 2].bitcast(F16),
                                        ALU.subtract).then_inc(kv_lo, 1)
                dve.wait_ge(kv_hi, b * (G + 2) + G + 2)
                tail = slice(P - TAIL, P)
                nc.vector.scalar_tensor_tensor(tmp[tail, 1, D // 2:D].bitcast(F16), s_bank[2][tail, :], mask[tail, :],
                                               tmp[tail, 1, 0:D // 2].bitcast(F16), ALU.mult, ALU.subtract).then_inc(kv_lo, 1)

            def moments(which, i, t, src):
                n = i * TT + t + 1
                nc.vector.bn_stats(stats[:, which, t, :], src).then_inc(bn_ready[which], 1)
                dve.wait_ge(bn_ready[which], n)
                nc.vector.tensor_tensor(nm[:, which, t:t + 1], stats[:, which, t, 1:2], stats[:, which, t, 4:5], ALU.add).then_inc(sum_ready[which], 1)
                nc.vector.bn_aggr(mv[:, which, t, :], stats[:, which, t, :]).then_inc(aggr_ready[which], 1)
                dve.wait_ge(aggr_ready[which], n)
                dve.wait_ge(sum_ready[which], n)
                nc.vector.tensor_scalar(nm[:, which, t:t + 1], nm[:, which, t:t + 1], -0.5, None, ALU.mult).then_inc(mean_ready[which], 1)

            def moments1(i, t, first=False):
                dve.wait_ge(xa_loaded[t], 16 * (i + 1))
                moments(0, i, t, x_tile(t, first))

            weight_low(range(2 * C))
            for t in range(TT):
                moments1(0, t, True)
            weight_low(range(2 * C, EARLY_UNITS))
            kv_low(0)
            with dve.Fori(1, B) as b:
                kv_low(b)
            dve.wait_ge(gates_ready, 1)
            nc.vector.tensor_scalar(gate[:, 2:3], gate_tanh[:, 0:1], 1.0, None, ALU.mult).then_inc(dve_small, 1)
            nc.vector.tensor_scalar(gate[:, 3:4], gate_tanh[:, 1:2], 0.5, None, ALU.mult).then_inc(dve_small, 1)
            dve.wait_ge(dve_small, 3)
            dve.wait_ge(consts_ready, 1)
            dve.wait_ge(small_loaded, 64)

            def xT_low(i, t):
                dve.wait_ge(xT_hi, i * TT + t + 1)
                cols = slice(P * t, P * t + P)
                src = xT_bank[t][:, :].rearrange("p (c n) -> p c n", c=C)
                nc.vector.tensor_tensor(buf1[:, LO, :, cols], src, buf1[:, HI, :, cols].bitcast(F32), ALU.subtract).then_inc(xT_lo, 1)

            def reduce_max(i, n):
                if n == 0:
                    later(dve, mT_done, i)
                dve.wait_ge(max_done, i * MAX_UNITS + n + 1)
                g, t = n // (TT + 1), n % (TT + 1)
                if t < TT:
                    nc.vector.reduce_max(mm[:, t, 4 * g:4 * g + 4], max_bank[n][:, :].rearrange("p (h s) -> p h s", h=4), AX.X).then_inc(reduced, 1)
                else:
                    nc.vector.reduce_max(mx[:, :, 4 * g:4 * g + 4], max_bank[n][:, :].rearrange("p (t h s) -> p t h s", t=TT, h=4), AX.X).then_inc(reduced, 1)

            def whole_max(i):
                dve.wait_ge(reduced, (i + 1) * MAX_UNITS)
                nc.vector.tensor_tensor(mm[:, :, 0:H], mm[:, :, 0:H], mx[:, :, :], ALU.max).then_inc(mm_ready, 1)

            def p_low(i, g, n):
                dve.wait_ge(p_full, i * 5 * G + 5 * g + n + 1)
                nc.vector.tensor_tensor(pq[:, n, LO, :], p32[(5 * g + n) % 2], pq[:, n, HI, :], ALU.subtract).then_inc(p_lo, 1)

            def attend(i, g):
                dve.wait_ge(av_done, i * G + g + 1)
                if g:
                    dve.wait_ge(attn_lo, i * G + g)
                nc.vector.reciprocal(tmp[:, 0, :], d_bank[:, :]).then_inc(recip_ready, 1)
                dve.wait_ge(recip_ready, i * G + g + 1)
                nc.vector.tensor_tensor(tmp[:, 0, :], o_bank[:, :], tmp[:, 0, :], ALU.mult).then_inc(attn32_ready, 1)

            def output(i, t):
                dve.wait_ge(th_ready, i * TT + t + 1)
                dve.wait_ge(v_done, i * TT + t + 1)
                nc.vector.scalar_tensor_tensor(th[:, :], th[:, :], 1.0, g_bank[V_BANK[t]][:, :], ALU.add, ALU.mult).then_inc(u_ready, 1)
                dve.wait_ge(u_ready, i * TT + t + 1)
                nc.vector.scalar_tensor_tensor(x1[:, t, :], th[:, :], gate[:, 3:4], x1[:, t, :], ALU.mult, ALU.add).then_inc(out_ready, 1)

            def residual(i, t):
                dve.wait_ge(x1_loaded[t], 16 * (i + 1))
                dve.wait_ge(wo_done, i * TT + t + 1)
                nc.vector.scalar_tensor_tensor(x1[:, t, :], g_bank[WO_BANK[t]][:, :], gate[:, 2:3], x1[:, t, :], ALU.mult, ALU.add).then_inc(x1_ready, 1)
                dve.wait_ge(x1_ready, i * TT + t + 1)
                moments(1, i, t, x1[:, t, :])

            def first_column(i):
                dve.wait_ge(av_done, (i + 1) * G)
                dve.wait_ge(p_lo, (i + 1) * 5 * G)
                later(dve, carry_ready, i)
                nc.vector.tensor_scalar(x2[:, :, 0], carry[:, :], flag[:, bass.ds(i, 1)], None, ALU.mult).then_inc(x2_first, 1)

            def keep_carry(i):
                dve.wait_ge(x2_ready, (i + 1) * TT)
                dve.wait_ge(x2_first, i + 1)
                nc.vector.tensor_copy(carry[:, :], x2[:, :, N]).then_inc(carry_ready, 1)

            def mix_k(i, c, pre):
                dve.wait_ge(diff_ready, i * C + c + 1)
                if c == 2 and pre:
                    dve.wait_ge(xT_done, (i + 2) * TT)
                if c == 3:
                    dve.wait_ge(*((q_lo, (i + 2) * G) if pre else (attn_lo, (i + 1) * G)))
                nc.vector.scalar_tensor_tensor(xk32[c], diff[c], mu[:, 1, c:c + 1], x2[:, c, 0:N], ALU.mult, ALU.add).then_inc(xk_mixed, 1)

            def mix_r(i, c):
                dve.wait_ge(xk_mixed, i * C + c + 1)
                nc.vector.scalar_tensor_tensor(diff[c], diff[c], mu[:, 0, c:c + 1], x2[:, c, 0:N], ALU.mult, ALU.add).then_inc(xr_mixed, 1)

            def mix_low(i, dst, c, src, hi_ready, lo_ready):
                dve.wait_ge(hi_ready, i * C + c + 1)
                low(dst[:, LO, c, :], src[c], dst[:, HI, c, :], lo_ready[1])

            def xk(i, pre):
                for c in range(3):
                    mix_k(i, c, pre)
                mix_low(i, buf3, 0, xk32, xk_hi, xk_lo)
                mix_k(i, 3, pre)
                mix_low(i, buf3, 3, xk32, xk_hi, xk_lo)

            def xr(i):
                for c in range(C):
                    mix_r(i, c)
                for c in (0, 3):
                    mix_low(i, buf2, c, diff, xr_hi, xr_lo)

            for t in range(TT):
                xT_low(0, t)
            for n in range(MAX_UNITS):
                reduce_max(0, n)
            whole_max(0)

            def step(i, ffn, pre):
                if ffn:
                    xr(i - 1)
                for n in range(5):
                    p_low(i, 0, n)
                if not ffn:
                    weight_low(range(EARLY_UNITS, EARLY_UNITS + C))
                if ffn:
                    dve.wait_ge(k2_lo, i * C)
                for g in range(1, G):
                    p_low(i, g, 0)
                    p_low(i, g, 1)
                    p_low(i, g, 2)
                    attend(i, g - 1)
                    p_low(i, g, 3)
                    p_low(i, g, 4)
                    if ffn:
                        output(i - 1, g - 1)
                    else:
                        weight_low(range(EARLY_UNITS + C * g, EARLY_UNITS + C * g + C))
                    if pre:
                        moments1(i + 1, g - 1)
                attend(i, G - 1)
                if ffn:
                    output(i - 1, TT - 1)
                first_column(i)
                if pre:
                    for t in range(3):
                        xT_low(i + 1, t)
                    moments1(i + 1, 3)
                for t in range(TT):
                    if t == TT - 1 and pre:
                        xT_low(i + 1, 3)
                    residual(i, t)
                if pre:
                    for n in range(MAX_UNITS):
                        reduce_max(i + 1, n)
                    whole_max(i + 1)
                keep_carry(i)
                xk(i, pre)

            step(0, False, True)
            with dve.Fori(1, BLOCKS - 1) as i:
                step(i, True, True)
            step(BLOCKS - 1, True, False)
            xr(BLOCKS - 1)
            for t in range(TT):
                output(BLOCKS - 1, t)

        @block.tensor
        def _(pe):
            def product(dst, stationary, moving, chunks, before=None):
                for c in range(chunks):
                    if before:
                        before(c)
                    for n, (s, m) in enumerate(PRODUCTS):
                        ins = nc.tensor.matmul(dst, stationary(s, c), moving(m, c), start=(c, n) == (0, 0),
                                               stop=(c, n) == (chunks - 1, len(PRODUCTS) - 1))
                return ins

            def transposed(dst, tiles):
                for n, tile in enumerate(tiles):
                    ins = nc.tensor.transpose(dst[:, P * n:P * n + P], tile, ident[:, :])
                return ins

            def cols(n):
                return slice(P * n, P * n + P)

            def weights_transposed(units):
                for u in units:
                    pe.wait_ge(nat_loaded[nat_place(u)], 16 * nat_loads(u))
                    if EARLY_UNITS <= u < EARLY_UNITS + 3:
                        pe.wait_ge(q_copied, 2 + u - EARLY_UNITS)
                    elif u >= 3:
                        pe.wait_ge(w_lo, u - 2)
                    transposed(g_bank[u % 3], [nat(u)[:, cols(c)] for c in range(C)]).then_inc(w_transposed, 1)

            def keys_values(b):
                pe.wait_ge(ctx_loaded, 32 * b + 32)
                later(pe, ctx_lo, 2 * b)
                for m in range(2):
                    transposed(ctx_bank[m], [ctx_nat[:, m, cols(c)] for c in range(C)]).then_inc(ctx_transposed, 1)
                pe.wait_ge(ctx_lo, 2 * b + 2)
                later(pe, kv_lo, (G + 2) * b)
                for g in range(G):
                    if g == 3:
                        pe.wait_ge(kv_lo, (G + 2) * b + 1)
                    product(s_bank[g % 3][:, 0:2 * P], lambda s, c: buf1[:, s, c, cols(g)], lambda m, c: buf3[:, m, c, 0:2 * P],
                            C).then_inc(kv_done, 1)
                for n in range(2):
                    pe.wait_ge(kv_lo, (G + 2) * b + 2 + n)
                    product(s_bank[1 + n][:, :], lambda s, c: buf3[:, s, c, cols(n)], lambda m, c: buf2[:, m, c, :],
                            C).then_inc(kv_done, 1)

            pe.wait_ge(ident_ready, 1)
            weights_transposed(range(EARLY_UNITS))
            pe.wait_ge(w_lo, EARLY_UNITS)
            keys_values(0)
            with pe.Fori(1, B) as b:
                keys_values(b)

            def xT(i, t, first=False):
                pe.wait_ge(xn1_ready, i * TT + t + 1)
                transposed(xT_bank[t], [x_tile(t, first)[:, cols(c)] for c in range(C)]).then_inc(xT_done, 1)

            def maximum(i, n):
                g, t = n // (TT + 1), n % (TT + 1)
                if n == 0:
                    pe.wait_ge(kv_loaded, 16 * KV_LOADS * (i + 1))
                if t == 0:
                    pe.wait_ge(q_hi, i * G + g + 1)
                if n >= 3:
                    pe.wait_ge(reduced, i * MAX_UNITS + n - 2)
                else:
                    later(pe, p_full, i * SCORE_UNITS)
                bank = max_bank[n]
                if t < TT:
                    ins = nc.tensor.matmul(bank[:, :], buf4[:, HI, g, cols(t)], k_pad[:, HI, g, :, :].rearrange("p j s -> p (j s)"),
                                           start=True, stop=True)
                else:
                    for e in range(TT):
                        ins = nc.tensor.matmul(bank[:, cols(e)], buf4[:, HI, g, cols(e)],
                                               k_tail[:, HI, g, :, :].rearrange("p j s -> p (j s)"), start=True, stop=True)
                ins.then_inc(max_done, 1)

            def query(i, g):
                def before(c):
                    n = (TT + 1) * (g - 1) + c - 1
                    if n >= 0:
                        maximum(i, n)

                if g == 0:
                    pe.wait_ge(xT_lo, (i + 1) * TT)
                product(g_bank[Q_BANK[g]][:, :], lambda s, c: WqT[:, s, c, cols(g)], lambda m, c: buf1[:, m, c, :], C,
                        before).then_inc(q_done, 1)
                before(C)

            def maxima_left(i):
                for n in range((TT + 1) * (G - 1) - 1, MAX_UNITS):
                    maximum(i, n)

            def maxima_transposed(i):
                pe.wait_ge(mm_ready, i + 1)
                later(pe, x2_ready, i * TT - 1)
                transposed(mT_bank, [mm[:, t, :] for t in range(TT)]).then_inc(mT_done, 1)

            def score(i, g, n):
                for k, (s, q) in enumerate(PRODUCTS):
                    keys = k_pad[:, s, g, n, :] if n < 4 else k_tail[:, s, g, :, :].rearrange("p j s -> p (j s)")
                    nc.tensor.matmul(score_bank[5 * g + n][:, :], keys, buf4[:, q, g, :], start=k == 0, stop=False)

            def less_maximum(g, n):
                if n < 4:
                    shift = negsel[:, 4 * g + n, 0:1].to_broadcast([P, P])
                else:
                    shift = negsel[:, 4 * g:4 * g + 4, :].rearrange("p h s -> p (h s)")
                nc.tensor.matmul(score_bank[5 * g + n][:, :], shift, mT[:, :], start=False, stop=True).then_inc(scores_done, 1)

            def first_scores(i):
                pe.wait_ge(q_lo, (i + 1) * G)
                for n in range(3):
                    if n == 2:
                        maxima_transposed(i)
                    pe.wait_ge(reduced, (i + 1) * MAX_UNITS - 2 + n)
                    score(i, 0, n)
                pe.wait_ge(mT_ready, i + 1)
                for n in range(3):
                    less_maximum(0, n)

            def scores(i, g, units):
                for n in units:
                    pe.wait_ge(p_full, i * SCORE_UNITS + 5 * g + n - 2)
                    score(i, g, n)
                    less_maximum(g, n)

            def values(i, g):
                pe.wait_ge(p_lo, i * SCORE_UNITS + 5 * g + 5)
                later(pe, attn32_ready, i * G + g)
                if g == 0:
                    later(pe, x2_ready, i * TT)
                for n in range(2):
                    for k, (s, q) in enumerate(PRODUCTS):
                        for j in range(4):
                            v = v_main[:, s, DH * (4 * g + j):DH * (4 * g + j + 1)] if n == 0 else v_tail[:, s, g, j, :]
                            nc.tensor.matmul(o_bank[DH * j:DH * j + DH, :], v, pq[:, 4 if n else j, q, :],
                                             start=(n, k) == (0, 0), stop=(n, k) == (1, 2))
                for n in range(2):
                    for q in (HI, LO):
                        for j in range(4):
                            one = ones_main[:, :] if n == 0 else ones_tail[:, j, :]
                            ins = nc.tensor.matmul(d_bank[DH * j:DH * j + DH, :], one, pq[:, 4 if n else j, q, :],
                                                   start=(n, q) == (0, HI), stop=(n, q) == (1, LO))
                ins.then_inc(av_done, 1)

            def project(i, t):
                def whole(c):
                    if t == 0:
                        pe.wait_ge(attn_lo, i * G + c + 1)

                product(g_bank[WO_BANK[t]][:, :], lambda s, c: buf3[:, s, c, cols(t)], lambda m, c: WoT[:, m, c, :], C, whole).then_inc(wo_done, 1)

            def x2_transposed(i, t):
                pe.wait_ge(xn2_ready, i * TT + t + 1)
                if t < 2:
                    pe.wait_ge(attn32_ready, (i + 1) * G)
                else:
                    pe.wait_ge(x2_ready, i * TT + t - 1)
                transposed(x2_bank[t], [xa[:, 1 + t % 2, cols(c)] for c in range(C)]).then_inc(x2_done, 1)

            def ffn_k(i, outs, queries=True):
                for c in outs:
                    if c == 3:
                        pe.wait_ge(relu_ready, i * C + 1)
                    elif queries:
                        pe.wait_ge(q_copied, (i + 1) * G + c + 2)
                for e in range(C):
                    wait_lo(pe, xk_lo, i, e)
                    for c in outs:
                        for n, (s, m) in enumerate(PRODUCTS):
                            ins = nc.tensor.matmul(g_bank[K_BANK[c]][:, :], WkT2[:, s, e, cols(c)], buf3[:, m, e, :],
                                                   start=(e, n) == (0, 0), stop=(e, n) == (C - 1, len(PRODUCTS) - 1))
                        if e == C - 1:
                            ins.then_inc(k_done, 1)

            def ffn_r(i, t):
                if t == 0:
                    wait_lo(pe, xr_lo, i, 2)
                    wait_lo(pe, xr_lo, i, 3)
                pe.wait_ge(*((relu_ready, i * C + 2), (relu_ready, i * C + 4), (u_ready, i * TT + 1), (u_ready, i * TT + 2))[t])
                product(g_bank[R_BANK[t]][:, :], lambda s, c: buf2[:, s, c, cols(t)], lambda m, c: WrT[:, m, c, :], C).then_inc(r_done, 1)

            def ffn_v(i, t):
                if t == 0:
                    pe.wait_ge(k2_lo, (i + 1) * C)
                pe.wait_ge(*((relu_ready, i * C + 3), (th_ready, i * TT + 1), (th_ready, i * TT + 2), (th_ready, i * TT + 3))[t])
                product(g_bank[V_BANK[t]][:, :], lambda s, c: buf1[:, s, c, cols(t)], lambda m, c: WvT2[:, m, c, :], C).then_inc(v_done, 1)

            pe.wait_ge(kv_lo, (G + 2) * B)
            for t in range(TT):
                xT(0, t, True)
            for g in range(G):
                if g == 3:
                    pe.wait_ge(q_copied, 1)
                query(0, g)
            maxima_left(0)

            def step(i, ffn, pre):
                first_scores(i)
                if ffn:
                    ffn_k(i - 1, (0, 1, 2))
                scores(i, 0, (3, 4))
                if ffn:
                    ffn_k(i - 1, (3,))
                else:
                    weights_transposed(range(EARLY_UNITS, EARLY_UNITS + C))
                for g in range(1, G):
                    scores(i, g, (0, 1, 2))
                    values(i, g - 1)
                    if ffn:
                        ffn_r(i - 1, g - 1)
                    scores(i, g, (3, 4))
                    if ffn:
                        ffn_v(i - 1, g - 1)
                    else:
                        weights_transposed(range(EARLY_UNITS + C * g, EARLY_UNITS + C * g + C))
                if ffn:
                    ffn_r(i - 1, TT - 1)
                values(i, G - 1)
                if ffn:
                    ffn_v(i - 1, TT - 1)
                if pre:
                    for t in range(3):
                        xT(i + 1, t)
                for t in range(TT):
                    if t < 3 and ffn:
                        pe.wait_ge(*((u_ready, i * TT - 1), (th_ready, i * TT), (u_ready, i * TT))[t])
                    elif t == 0:
                        pe.wait_ge(w_lo, ALL_UNITS)
                    if t == 3:
                        if pre:
                            pe.wait_ge(x1_ready, i * TT + 1)
                            xT(i + 1, 3)
                        pe.wait_ge(x1_ready, i * TT + 2)
                    project(i, t)
                x2_transposed(i, 0)
                x2_transposed(i, 1)
                for g in range(G):
                    if pre:
                        pe.wait_ge(*((x1_ready, i * TT + 3), (xT_lo, (i + 2) * TT), (x1_ready, i * TT + 4), (q_copied, (i + 1) * G + 1))[g])
                        query(i + 1, g)
                    if g < 2:
                        x2_transposed(i, 2 + g)
                if pre:
                    maxima_left(i + 1)

            step(0, False, True)
            with pe.Fori(1, BLOCKS - 1) as i:
                step(i, True, True)
            step(BLOCKS - 1, True, False)
            pe.wait_ge(x1_ready, BLOCKS * TT)
            ffn_k(BLOCKS - 1, (0, 1, 2), queries=False)
            ffn_k(BLOCKS - 1, (3,))
            for t in range(TT):
                ffn_r(BLOCKS - 1, t)
                ffn_v(BLOCKS - 1, t)


NAMES = ("x", "ctx_1024", "g_xattn", "g_ffn", "L0_xattn_Wq", "L0_xattn_Wk", "L0_xattn_Wv", "L0_xattn_Wo",
         "L0_ffn_W_r", "L0_ffn_W_k", "L0_ffn_W_v", "L0_ffn_mu_r", "L0_ffn_mu_k")


def kernel(**inputs):
    import numpy as np
    import concourse.bacc as bacc
    from concourse.bass_utils import run_bass_kernel_spmd

    nc = bacc.Bacc("TRN2", target_bir_lowering=False, num_devices=1)
    arrays, args = {}, []
    for name in NAMES:
        a = np.ascontiguousarray(inputs[name])
        arrays[f"in_{name}"] = a
        args.append(nc.dram_tensor(f"in_{name}", a.shape, mybir.dt.from_np(a.dtype), kind="ExternalInput").ap())
    out = nc.dram_tensor("out_0", arrays["in_x"].shape, F32, kind="ExternalOutput").ap()
    flamingo_block(nc, *args, out)
    return run_bass_kernel_spmd(nc, [arrays], core_ids=[0]).results[0]["out_0"]
```

```python
from contextlib import ExitStack

import concourse.bass as bass
from concourse import mybir

F32 = mybir.dt.float32
F32R = mybir.dt.float32r
F16 = mybir.dt.float16
ALU = mybir.AluOpType
ACT = mybir.ActivationFunctionType
AX = mybir.AxisListType

HI, LO = 0, 1
PRODUCTS = ((HI, HI), (HI, LO), (LO, HI))


def flamingo_block(nc, x, ctx_tokens, g_xattn, g_ffn, Wq, Wk, Wv, Wo, W_r, W_k, W_v, mu_r, mu_k, out):
    B, T, D = x.shape
    S = ctx_tokens.shape[1]
    H = 16
    DH = D // H
    P = 128
    C = D // P
    G = H // 4
    N = 512
    TT = N // P
    BLOCKS = B * T // N
    PER_BATCH = T // N
    TAIL = 32
    OVER = P + TAIL - S
    SCALE = float(DH) ** -0.5
    EPS = 1e-5
    assert D == C * P == 512 and DH == 32 and C == G == TT and P < S <= P + TAIL and T % N == 0 and B == 4

    x_tiles = x.rearrange("b (n t p) d -> (b n) t p d", t=TT, p=P)
    out_tiles = out.rearrange("b (n t p) d -> (b n) t p d", t=TT, p=P)

    k_scratch = nc.dram_tensor("k_scratch", [B, P, 2, G, P], F32, kind="Internal").ap()
    kt_scratch = nc.dram_tensor("kt_scratch", [P, 2, G, B * TAIL], F32, kind="Internal").ap()
    v_scratch = nc.dram_tensor("v_scratch", [B, P, 2, D], F16, kind="Internal").ap()
    vt_scratch = nc.dram_tensor("vt_scratch", [B, TAIL, 2, D], F16, kind="Internal").ap()

    with ExitStack() as ctx:
        def sb(name, shape, dt):
            return ctx.enter_context(nc.sbuf_tensor(name, shape, dt))

        def psum(name):
            return ctx.enter_context(nc.psum_tensor(name, [P, 512], F32))

        def sem(name):
            return ctx.enter_context(nc.semaphore(name))

        WqT, WoT, WrT, WkT2, WvT2 = (sb(n, [P, 2, C, D], F32R) for n in ("WqT", "WoT", "WrT", "WkT2", "WvT2"))
        buf1 = sb("buf1", [P, 2, C, N], F32R)
        buf2 = sb("buf2", [P, 2, C, N], F32R)
        buf3 = sb("buf3", [P, 2, C, N], F32R)
        buf4 = sb("buf4", [P, 2, C, N], F32R)
        k_pad = sb("k_pad", [P, 2, G, 4, P], F32R)
        k_tail = sb("k_tail", [P, 2, G, 4, TAIL], F32R)
        v_main = sb("v_main", [P, 2, D], F16)
        v_tail = sb("v_tail", [P, 2, G, 4, TAIL], F16)
        ones_main = sb("ones_main", [P, DH], F16)
        ones_tail = sb("ones_tail", [P, 4, DH], F16)
        xa = sb("xa", [P, 3, D], F32)
        x1 = sb("x1", [P, TT, D], F32)
        ring = sb("ring", [P, C * (N + 1) + 2 * N], F32)
        tmp = sb("tmp", [P, 2, N], F32)
        th = sb("th", [P, N], F32)
        mm = sb("mm", [P, TT, P], F32)
        mT = sb("mT", [P, N], F32R)
        mx = sb("mx", [P, TT, H], F32)
        ident = sb("ident", [P, P], F32)
        negsel = sb("negsel", [P, H, TAIL], F32R)
        mask = sb("mask", [P, 1], F32)
        minus_half = sb("minus_half", [P, 1], F32)
        flag = sb("flag", [P, BLOCKS], F32)
        carry = sb("carry", [P, C], F32)
        mu = sb("mu", [P, 2, C], F32)
        gate = sb("gate", [P, 4], F32)
        gate_tanh = sb("gate_tanh", [P, 2], F32)
        stats = sb("stats", [P, 2, TT, 6], F32)
        mv = sb("mv", [P, 2, TT, 2], F32)
        nm = sb("nm", [P, 2, TT], F32)
        ve = sb("ve", [P, 2, TT], F32)
        rstd = sb("rstd", [P, 2, TT], F32)
        nb = sb("nb", [P, 2, TT], F32)
        eps = sb("eps", [P, 1], F32)

        p32 = (ring[:, 0:N], tmp[:, 1, :])
        pq = ring[:, N:6 * N].bitcast(F16).rearrange("p (c s n) -> p c s n", c=5, s=2)
        X2W = N + 1
        x2 = ring[:, 0:C * X2W].rearrange("p (c n) -> p c n", c=C)
        k2 = (tmp[:, 0, :], th[:, :])
        diff = (th[:, :], xa[:, 1, :], xa[:, 2, :], tmp[:, 1, :])
        xk32 = (ring[:, C * X2W:C * X2W + N], ring[:, C * X2W + N:C * X2W + 2 * N], xa[:, 0, :], tmp[:, 0, :])

        s_bank = [psum(f"s_bank{n}") for n in range(3)]
        o_bank, d_bank = psum("o_bank"), psum("d_bank")
        g_bank = [psum(f"g_bank{n}") for n in range(3)]

        ident_ready, heads_ready, tails_ready, mask_ready, consts_ready = (
            sem(n) for n in ("ident_ready", "heads_ready", "tails_ready", "mask_ready", "consts_ready"))
        chain = sem("chain")
        small_loaded = sem("small_loaded")
        gates_ready = sem("gates_ready")
        nat_loaded = [sem(f"nat_loaded{n}") for n in range(8)]
        w_transposed = sem("w_transposed")
        w_hi = sem("w_hi")
        w_lo = sem("w_lo")
        ctx_loaded = sem("ctx_loaded")
        ctx_transposed = sem("ctx_transposed")
        ctx_hi = sem("ctx_hi")
        ctx_lo = sem("ctx_lo")
        kv_done = sem("kv_done")
        kv_hi = sem("kv_hi")
        kv_lo = sem("kv_lo")
        kv_stored = [sem(f"kv_stored{n}") for n in range(3)]
        kv_loaded = sem("kv_loaded")
        xa_loaded = [sem(f"xa_loaded{t}") for t in range(TT)]
        x1_loaded = [sem(f"x1_loaded{t}") for t in range(TT)]
        out_stored = [sem(f"out_stored{t}") for t in range(TT)]
        bn_ready, sum_ready, aggr_ready, mean_ready, var_eps_ready, rstd_ready, norm_ready = (
            [sem(f"{n}{which}") for which in (1, 2)]
            for n in ("bn_ready", "sum_ready", "aggr_ready", "mean_ready", "var_eps_ready", "rstd_ready", "norm_ready"))
        dve_small = sem("dve_small")
        xn1_ready = sem("xn1_ready")
        xn2_ready = sem("xn2_ready")
        xT_done, xT_hi, xT_lo = sem("xT_done"), sem("xT_hi"), sem("xT_lo")
        q_done, q_hi, q_copied, q_lo = sem("q_done"), sem("q_hi"), sem("q_copied"), sem("q_lo")
        max_done = sem("max_done")
        reduced = sem("reduced")
        mm_ready, mT_done, mT_ready = sem("mm_ready"), sem("mT_done"), sem("mT_ready")
        scores_done = sem("scores_done")
        p_hi, p_full, p_lo = sem("p_hi"), sem("p_full"), sem("p_lo")
        av_done = sem("av_done")
        recip_ready, attn32_ready = sem("recip_ready"), sem("attn32_ready")
        attn_hi, attn_lo = sem("attn_hi"), sem("attn_lo")
        wo_done, x1_ready = sem("wo_done"), sem("x1_ready")
        x2_done, x2_ready = sem("x2_done"), sem("x2_ready")
        x2_first, carry_ready = sem("x2_first"), sem("carry_ready")
        diff_ready = sem("diff_ready")
        xk_mixed, xk_hi = sem("xk_mixed"), sem("xk_hi")
        xr_mixed, xr_hi = sem("xr_mixed"), sem("xr_hi")
        xk_lo, xr_lo = ([sem(n + "_lo12"), sem(n + "_lo03")] for n in ("xk", "xr"))
        k_done, relu_ready, k2_ready, k2_hi, k2_lo = (sem(n) for n in ("k_done", "relu_ready", "k2_ready", "k2_hi", "k2_lo"))
        r_done, th_ready, v_done, u_ready, out_ready = (sem(n) for n in ("r_done", "th_ready", "v_done", "u_ready", "out_ready"))
        WO_BANK, Q_BANK = (0, 1, 2, 1), (2, 0, 1, 2)
        K_BANK, R_BANK, V_BANK = (0, 1, 2, 0), (1, 0, 2, 1), (2, 1, 0, 2)
        SCORE_UNITS, MAX_UNITS = G * 5, TT * G + TT
        score_bank = [d_bank] + [s_bank[m % 3] for m in range(1, SCORE_UNITS)]
        max_bank = [s_bank[(SCORE_UNITS + n) % 3] for n in range(MAX_UNITS)]
        xT_bank = s_bank + [g_bank[0]]
        x2_bank = [(o_bank, d_bank)[t % 2] for t in range(TT)]
        mT_bank = o_bank
        KV_LOADS = 13

        early = ((Wk, buf1), (Wv, buf2), (Wq, WqT))
        late = ((Wo, WoT), (W_k, WkT2), (W_r, WrT), (W_v, WvT2))
        weights = early + late
        EARLY_UNITS, ALL_UNITS = C * len(early), C * len(weights)
        ring_nat = ring[:, 0:C * D].rearrange("p (c n) -> p c n", c=C)

        def late_units(n):
            return range(EARLY_UNITS + 3 * n, min(EARLY_UNITS + 3 * n + 3, ALL_UNITS))

        def nat_place(u):
            return u % 8 if u < EARLY_UNITS else u % 4

        def nat(u):
            place = nat_place(u)
            return x1[:, place, :] if place < 4 else ring_nat[:, place - 4, :]

        def nat_loads(u):
            return sum(nat_place(v) == nat_place(u) for v in range(u + 1))

        ctx_nat = ring[:, C * D:C * D + 2 * D].rearrange("p (m n) -> p m n", m=2)
        ctx_bank = (o_bank, d_bank)

        TILES, COLUMN = (1, 2, 2), (0, 2 * P, 0)
        FIRST_TILE, FIRST_UNIT = (0, 1, 3), (0, G + 1, 2 * G + 3)
        KV_UNITS = 3 * G + 5
        v_stage = [place.bitcast(F16).rearrange("p (s n) -> p s n", s=2) for place in (ring_nat[:, 0, :], tmp[:, 0, :], tmp[:, 1, :])]

        def v_place(item, m):
            return v_stage[m + (item > 0)]

        def x_tile(t, first=False):
            return th[:, :] if first and t == 3 else xa[:, t % 3, :]

        block = ctx.enter_context(nc.Block())

        def wait_lo(eng, pair, i, c):
            later(eng, pair[c in (0, 3)], 2 * i + 1 + c // 2)

        def later(eng, semaphore, value):
            if not isinstance(value, int) or value > 0:
                eng.wait_ge(semaphore, value)

        @block.sync
        def _(sp):
            def load_weight(u):
                if u >= EARLY_UNITS:
                    sp.wait_ge(w_transposed, u - 3)
                elif u >= 8:
                    sp.wait_ge(w_transposed, u - 7)
                sp.dma_start(nat(u), weights[u // C][0][P * (u % C):P * (u % C) + P, :]).then_inc(nat_loaded[nat_place(u)], 16)

            def load_tails():
                for b in range(B):
                    sp.dma_start(ctx_nat[TAIL * b:TAIL * b + TAIL, 0, :], ctx_tokens[b, S - TAIL:S, :]).then_inc(ctx_loaded, 16)

            def load_mains(item):
                sp.wait_ge(ctx_transposed, FIRST_TILE[item])
                for m in range(2):
                    sp.dma_start(ctx_nat[:, m, :], ctx_tokens[2 * (item - 1) + m, 0:P, :]).then_inc(ctx_loaded, 16)

            def store_kv(item):
                units = FIRST_UNIT[item] + G + TILES[item]
                sp.wait_ge(kv_lo, units)
                sp.wait_ge(kv_hi, units)
                if item == 0:
                    sp.dma_start(kt_scratch, buf4[:, :, :, 0:P].bitcast(F32)).then_inc(kv_stored[0], 16)
                    sp.dma_start(vt_scratch.rearrange("b r s n -> (b r) s n"), v_place(0, 0)).then_inc(kv_stored[0], 16)
                else:
                    for m in range(2):
                        b, col = 2 * (item - 1) + m, COLUMN[item] + P * m
                        sp.dma_start(k_scratch[b], buf4[:, :, :, col:col + P].bitcast(F32)).then_inc(kv_stored[item], 16)
                        sp.dma_start(v_scratch[b], v_place(item, m)).then_inc(kv_stored[item], 16)

            def load_xa(i, t, first=False):
                sp.dma_start(x_tile(t, first), x_tiles[i, t]).then_inc(xa_loaded[t], 16)

            def load_x1(i, t):
                later(sp, out_stored[t], 16 * i)
                sp.dma_start(x1[:, t, :], x_tiles[i, t]).then_inc(x1_loaded[t], 16)

            def load_kv(i, heads):
                later(sp, av_done, i * G)
                b = i // PER_BATCH
                for j in heads:
                    rows = slice(DH * j, DH * j + DH)
                    sp.dma_start(k_pad[rows, :, :, j, :].bitcast(F32), k_scratch[b, rows, :, :, :]).then_inc(kv_loaded, 16)
                    sp.dma_start(k_tail[rows, :, :, j, :].bitcast(F32), kt_scratch[rows, :, :, bass.ds(b * TAIL, TAIL)]).then_inc(kv_loaded, 16)
                    sp.dma_start(v_tail[rows, :, :, j, :], vt_scratch[b].rearrange("r s (g j d) -> r s g j d", g=G, j=4)[:, :, :, j, :]).then_inc(kv_loaded, 16)
                if 3 in heads:
                    sp.dma_start(v_main[:, :, :], v_scratch[b]).then_inc(kv_loaded, 16)

            def store_out(i, t):
                sp.wait_ge(out_ready, i * TT + t + 1)
                sp.dma_start(out_tiles[i, t], x1[:, t, :]).then_inc(out_stored[t], 16)

            for u in range(8):
                load_weight(u)
            load_tails()
            for col, g in enumerate((g_xattn, g_ffn)):
                sp.dma_start(gate[:, col:col + 1], g.rearrange("(a n) -> a n", a=1).to_broadcast([P, 1])).then_inc(small_loaded, 16)
            for n, m in enumerate((mu_r, mu_k)):
                sp.dma_start(mu[:, n, :], m.rearrange("(c p) -> p c", p=P), allow_slow_non_contiguous=True).then_inc(small_loaded, 16)
            for t in range(3):
                load_xa(0, t)
            sp.wait_ge(dve_small, 1)
            load_xa(0, 3, True)
            load_mains(1)
            for u in range(8, EARLY_UNITS):
                load_weight(u)
            store_kv(0)
            load_mains(2)
            for u in range(EARLY_UNITS, EARLY_UNITS + C):
                load_weight(u)
            store_kv(1)
            sp.wait_ge(consts_ready, 1)
            sp.wait_ge(kv_stored[0], 32)
            sp.wait_ge(kv_stored[1], 64)
            load_kv(0, range(4))
            store_kv(2)

            def step(i, ffn, pre):
                if pre:
                    sp.wait_ge(xT_done, (i + 1) * TT)
                    wait_lo(sp, xk_lo, i - 1, 2)
                    load_xa(i + 1, 0)
                    wait_lo(sp, xr_lo, i - 1, 2)
                    load_xa(i + 1, 1)
                    load_xa(i + 1, 2)
                if not ffn:
                    for u in range(EARLY_UNITS + C, ALL_UNITS):
                        load_weight(u)
                    sp.wait_ge(w_transposed, ALL_UNITS)
                for t in range(TT):
                    last = t == TT - 1 and pre
                    if last:
                        sp.wait_ge(xT_done, (i + 1) * TT + 1)
                        load_xa(i + 1, 3)
                        load_kv(i + 1, (0,))
                    if ffn:
                        store_out(i - 1, t)
                    if last:
                        load_kv(i + 1, (1,))
                    load_x1(i, t)
                    if last:
                        load_kv(i + 1, (2, 3))

            step(0, False, True)
            with sp.Fori(1, BLOCKS - 1) as i:
                step(i, True, True)
            step(BLOCKS - 1, True, False)
            for t in range(TT):
                store_out(BLOCKS - 1, t)
            for t in range(TT):
                sp.wait_ge(out_stored[t], 16 * BLOCKS)

        @block.gpsimd
        def _(pool):
            done = [0]

            def link(ins):
                done[0] += 1
                ins.then_inc(chain, 1)
                pool.wait_ge(chain, done[0])

            link(nc.gpsimd.memset(ident[:, :], 0.0))
            link(nc.gpsimd.affine_select(out=ident[:, :], in_=ident[:, :], compare_op=ALU.not_equal, fill=1.0,
                                         base=0, pattern=[[-1, P]], channel_multiplier=1))
            nc.gpsimd.memset(flag[:, :], 1.0).then_inc(ident_ready, 1)
            heads = th[:, :].rearrange("p (h s) -> p h s", h=H)
            link(nc.gpsimd.memset(heads, 0.0))
            link(nc.gpsimd.affine_select(out=heads, in_=heads, compare_op=ALU.not_equal, fill=-1.0,
                                         base=0, pattern=[[-1, H], [0, TAIL]], channel_multiplier=1))
            nc.gpsimd.memset(minus_half[:, :], -0.5).then_inc(heads_ready, 1)
            link(nc.gpsimd.memset(ones_main[:, :], 1.0))
            link(nc.gpsimd.memset(ones_tail[:, :, :], 1.0))
            link(nc.gpsimd.affine_select(out=ones_tail[:, :, :], in_=ones_tail[:, :, :], compare_op=ALU.is_ge, fill=0.0,
                                         base=-OVER, pattern=[[-DH, 4], [0, DH]], channel_multiplier=1))
            link(nc.gpsimd.affine_select(out=ones_tail[:, :, :], in_=ones_tail[:, :, :], compare_op=ALU.is_ge, fill=0.0,
                                         base=DH - 1, pattern=[[DH, 4], [0, DH]], channel_multiplier=-1))
            tail_rows = mx[:, 0, 0:B]
            link(nc.gpsimd.memset(tail_rows, 1.0))
            link(nc.gpsimd.affine_select(out=tail_rows, in_=tail_rows, compare_op=ALU.is_ge, fill=0.0,
                                         base=-OVER, pattern=[[-DH, B]], channel_multiplier=1))
            nc.gpsimd.affine_select(out=tail_rows, in_=tail_rows, compare_op=ALU.is_ge, fill=0.0,
                                    base=DH - 1, pattern=[[DH, B]], channel_multiplier=-1).then_inc(tails_ready, 1)
            pool.wait_ge(heads_ready, 1)
            link(nc.gpsimd.memset(eps[:, :], EPS))
            pool.wait_ge(ident_ready, 1)
            link(nc.gpsimd.memset(flag[:, 0:BLOCKS:PER_BATCH], 0.0))
            link(nc.gpsimd.memset(carry[:, :], 0.0))
            link(nc.gpsimd.memset(mm[:, :, :], 0.0))
            link(nc.gpsimd.memset(k_pad[:].bitcast(F32), 0.0))
            link(nc.gpsimd.memset(k_tail[:].bitcast(F32), 0.0))
            nc.gpsimd.memset(v_tail[:, :, :, :, :], 0.0).then_inc(consts_ready, 1)

            def norm(which, i, t):
                n = i * TT + t + 1
                pool.wait_ge(mean_ready[which], n)
                nc.gpsimd.tensor_tensor(ve[:, which, t:t + 1], mv[:, which, t, 1:2], eps[:, :], ALU.add).then_inc(var_eps_ready[which], 1)
                pool.wait_ge(var_eps_ready[which], n)
                nc.gpsimd.tensor_tensor(rstd[:, which, t:t + 1], ve[:, which, t:t + 1], minus_half[:, :], ALU.pow).then_inc(rstd_ready[which], 1)
                pool.wait_ge(rstd_ready[which], n)
                nc.gpsimd.tensor_tensor(nb[:, which, t:t + 1], nm[:, which, t:t + 1], rstd[:, which, t:t + 1], ALU.mult).then_inc(norm_ready[which], 1)

            def difference(i, c):
                if c == 0:
                    pool.wait_ge(x2_ready, i * TT + TT)
                    pool.wait_ge(x2_first, i + 1)
                    later(pool, out_ready, i * TT)
                if c == 3:
                    pool.wait_ge(p_lo, (i + 1) * SCORE_UNITS)
                nc.gpsimd.tensor_tensor(diff[c], x2[:, c, 1:N + 1], x2[:, c, 0:N], ALU.subtract).then_inc(diff_ready, 1)

            def mix_low(i, dst, c, src, hi_ready, lo_ready):
                pool.wait_ge(hi_ready, i * C + c + 1)
                nc.gpsimd.tensor_tensor(dst[:, LO, c, :], src[c], dst[:, HI, c, :].bitcast(F32), ALU.subtract).then_inc(lo_ready[0], 1)

            def q_low(i, g):
                pool.wait_ge(q_copied, i * G + g + 1)
                nc.gpsimd.tensor_tensor(buf4[:, LO, g, :], tmp[:, 0, :], buf4[:, HI, g, :].bitcast(F32), ALU.subtract).then_inc(q_lo, 1)

            def k2_low(i, c):
                pool.wait_ge(k2_hi, i * C + c + 1)
                nc.gpsimd.tensor_tensor(buf1[:, LO, c, :], k2[c % 2], buf1[:, HI, c, :].bitcast(F32), ALU.subtract).then_inc(k2_lo, 1)

            def attn_low(i, g):
                pool.wait_ge(attn_hi, i * G + g + 1)
                nc.gpsimd.tensor_tensor(buf3[:, LO, g, :], tmp[:, 0, :], buf3[:, HI, g, :].bitcast(F32), ALU.subtract).then_inc(attn_lo, 1)

            for t in range(TT):
                norm(0, 0, t)
            for g in range(G):
                q_low(0, g)

            def step(i, ffn, pre):
                if ffn:
                    for c in (1, 2):
                        mix_low(i - 1, buf2, c, diff, xr_hi, xr_lo)
                    for c in range(C):
                        k2_low(i - 1, c)
                for g in range(1, G):
                    attn_low(i, g - 1)
                    if pre:
                        norm(0, i + 1, g - 1)
                attn_low(i, G - 1)
                if pre:
                    norm(0, i + 1, 3)
                for t in range(TT):
                    norm(1, i, t)
                if pre:
                    q_low(i + 1, 0)
                    q_low(i + 1, 1)
                for c in range(C):
                    difference(i, c)
                    if c >= 2 and pre:
                        q_low(i + 1, c)
                for c in (1, 2):
                    mix_low(i, buf3, c, xk32, xk_hi, xk_lo)

            step(0, False, True)
            with pool.Fori(1, BLOCKS - 1) as i:
                step(i, True, True)
            step(BLOCKS - 1, True, False)
            for c in (1, 2):
                mix_low(BLOCKS - 1, buf2, c, diff, xr_hi, xr_lo)
            for c in range(C):
                k2_low(BLOCKS - 1, c)

        @block.scalar
        def _(act):
            def high(dst, src, done):
                nc.scalar.activation(dst, src, ACT.Copy).then_inc(done, 1)

            def weight_high(u):
                act.wait_ge(w_transposed, u + 1)
                high(weights[u // C][1][:, HI, :, P * (u % C):P * (u % C) + P], g_bank[u % 3][:, :].rearrange("p (c n) -> p c n", c=C), w_hi)

            def ctx_high(item):
                for m in range(TILES[item]):
                    col = COLUMN[item] + P * m
                    act.wait_ge(ctx_transposed, FIRST_TILE[item] + m + 1)
                    if item == 2:
                        act.wait_ge(kv_done, G + 1)
                    high(buf3[:, HI, :, col:col + P], ctx_bank[m][:, :].rearrange("p (c n) -> p c n", c=C), ctx_hi)

            def keys_high(item):
                width = P * TILES[item]
                for g in range(G):
                    u = FIRST_UNIT[item] + g
                    act.wait_ge(kv_done, u + 1)
                    if item == 2:
                        act.wait_ge(kv_stored[0], 32)
                    high(buf4[:, HI, g, COLUMN[item]:COLUMN[item] + width], s_bank[u % 3][:, 0:width], kv_hi)

            def values_high(item):
                for m in range(TILES[item]):
                    u = FIRST_UNIT[item] + G + m
                    act.wait_ge(kv_done, u + 1)
                    if item == 0:
                        act.wait_ge(mask_ready, 1)
                        nc.scalar.activation(v_place(0, 0)[:, HI, :], s_bank[u % 3][:, :], ACT.Copy, scale=mask[:, :]).then_inc(kv_hi, 1)
                    else:
                        if item == 2:
                            act.wait_ge(kv_stored[1], 64)
                        high(v_place(item, m)[:, HI, :], s_bank[u % 3][:, :], kv_hi)

            for u in range(2 * C):
                weight_high(u)
            ctx_high(0)
            keys_high(0)
            ctx_high(1)
            values_high(0)
            for u in range(2 * C, EARLY_UNITS):
                weight_high(u)

            def norm1(i, t, first=False):
                act.wait_ge(norm_ready[0], i * TT + t + 1)
                nc.scalar.activation(x_tile(t, first), x_tile(t, first), ACT.Identity, bias=nb[:, 0, t:t + 1],
                                     scale=rstd[:, 0, t:t + 1]).then_inc(xn1_ready, 1)

            act.wait_ge(small_loaded, 64)
            nc.scalar.activation(gate_tanh[:, 0:2], gate[:, 0:2], ACT.Tanh).then_inc(gates_ready, 1)
            keys_high(1)
            ctx_high(2)
            values_high(1)
            keys_high(2)
            for t in range(TT):
                norm1(0, t, True)
            values_high(2)

            def norm2(i, t, pre):
                if t >= 2:
                    act.wait_ge(x2_done, i * TT + t - 1)
                elif pre:
                    act.wait_ge(xT_done, (i + 1) * TT + t + 2)
                act.wait_ge(norm_ready[1], i * TT + t + 1)
                nc.scalar.activation(xa[:, 1 + t % 2, :], x1[:, t, :], ACT.Identity, bias=nb[:, 1, t:t + 1],
                                     scale=rstd[:, 1, t:t + 1]).then_inc(xn2_ready, 1)

            def xT_high(i, t):
                act.wait_ge(xT_done, i * TT + t + 1)
                later(act, v_done, (i - 1) * TT)
                high(buf1[:, HI, :, P * t:P * t + P], xT_bank[t][:, :].rearrange("p (c n) -> p c n", c=C), xT_hi)

            def q_high(i, g):
                act.wait_ge(q_done, i * G + g + 1)
                high(buf4[:, HI, g, :], g_bank[Q_BANK[g]][:, :], q_hi)
                if g:
                    act.wait_ge(q_lo, i * G + g)
                else:
                    later(act, attn_lo, i * G)
                high(tmp[:, 0, :], g_bank[Q_BANK[g]][:, :], q_copied)

            def k_relu(i, c):
                act.wait_ge(k_done, i * C + c + 1)
                if c >= 2:
                    act.wait_ge(k2_lo, i * C + c - 1)
                elif c == 1:
                    wait_lo(act, xr_lo, i, 0)
                else:
                    wait_lo(act, xk_lo, i, 3)
                nc.scalar.activation(k2[c % 2], g_bank[K_BANK[c]][:, :], ACT.Relu).then_inc(relu_ready, 1)

            def k_square(i, c):
                act.wait_ge(relu_ready, i * C + c + 1)
                nc.scalar.activation(k2[c % 2], k2[c % 2], ACT.Square).then_inc(k2_ready, 1)

            def k2_high(i, c):
                act.wait_ge(k2_ready, i * C + c + 1)
                high(buf1[:, HI, c, :], k2[c % 2], k2_hi)

            def relu_squared(i, c):
                k_relu(i, c)
                k_square(i, c)
                k2_high(i, c)

            def exps(i, g, n):
                u = i * 5 * G + 5 * g + n
                bank = score_bank[5 * g + n]
                act.wait_ge(scores_done, u + 1)
                if n == 0:
                    if g == 0:
                        wait_lo(act, xk_lo, i - 1, 0)
                        wait_lo(act, xk_lo, i - 1, 1)
                        later(act, xr_mixed, i * C)
                    later(act, av_done, i * G + g)
                nc.scalar.activation(pq[:, n, HI, :], bank[:, :], ACT.Exp, scale=SCALE).then_inc(p_hi, 1)
                m = 5 * g + n
                if m == 1:
                    wait_lo(act, xr_lo, i - 1, 3)
                if m >= 2:
                    act.wait_ge(p_lo, u - 1)
                nc.scalar.activation(p32[m % 2], bank[:, :], ACT.Exp, scale=SCALE).then_inc(p_full, 1)

            def tanh_r(i, t):
                act.wait_ge(r_done, i * TT + t + 1)
                if t:
                    act.wait_ge(out_ready, i * TT + t)
                else:
                    act.wait_ge(k2_lo, (i + 1) * C)
                nc.scalar.activation(th[:, :], g_bank[R_BANK[t]][:, :], ACT.Tanh, scale=0.5).then_inc(th_ready, 1)

            def attn_high(i, g):
                act.wait_ge(attn32_ready, i * G + g + 1)
                high(buf3[:, HI, g, :], tmp[:, 0, :], attn_hi)

            def x2_copy(i, t):
                act.wait_ge(x2_done, i * TT + t + 1)
                act.wait_ge(p_lo, (i + 1) * 5 * G)
                act.wait_ge(av_done, (i + 1) * G)
                nc.scalar.activation(x2[:, :, 1 + P * t:1 + P * t + P],
                                     x2_bank[t][:, :].rearrange("p (c n) -> p c n", c=C), ACT.Copy).then_inc(x2_ready, 1)

            def mix_high(i, dst, c, src, mixed_ready, hi_ready):
                act.wait_ge(mixed_ready, i * C + c + 1)
                high(dst[:, HI, c, :], src[c], hi_ready)

            def mT_copy(i):
                act.wait_ge(mT_done, i + 1)
                high(mT[:, :], mT_bank[:, :], mT_ready)

            act.wait_ge(kv_done, KV_UNITS)
            for t in range(TT):
                xT_high(0, t)
            act.wait_ge(kv_stored[1], 64)
            act.wait_ge(kv_stored[2], 64)
            for g in range(G):
                q_high(0, g)
            mT_copy(0)

            def step(i, ffn, pre):
                if ffn:
                    for c in range(C):
                        mix_high(i - 1, buf2, c, diff, xr_mixed, xr_hi)
                else:
                    for u in late_units(0):
                        weight_high(u)
                for n in range(4):
                    exps(i, 0, n)
                if ffn:
                    relu_squared(i - 1, 0)
                exps(i, 0, 4)
                if ffn:
                    relu_squared(i - 1, 1)
                    relu_squared(i - 1, 2)
                    relu_squared(i - 1, 3)
                else:
                    for u in late_units(1):
                        weight_high(u)
                for g in range(1, G):
                    exps(i, g, 0)
                    exps(i, g, 1)
                    exps(i, g, 2)
                    if ffn:
                        tanh_r(i - 1, g - 1)
                    exps(i, g, 3)
                    exps(i, g, 4)
                    attn_high(i, g - 1)
                    if not ffn:
                        for u in late_units(1 + g):
                            weight_high(u)
                    if g >= 2 and pre:
                        norm1(i + 1, g - 2)
                if pre:
                    norm1(i + 1, 2)
                if ffn:
                    tanh_r(i - 1, TT - 1)
                else:
                    for u in late_units(1 + G):
                        weight_high(u)
                attn_high(i, G - 1)
                if pre:
                    for t in range(3):
                        xT_high(i + 1, t)
                    norm1(i + 1, 3)
                norm2(i, 0, pre)
                if pre:
                    xT_high(i + 1, 3)
                norm2(i, 1, pre)
                x2_copy(i, 0)
                norm2(i, 2, pre)
                x2_copy(i, 1)
                if pre:
                    q_high(i + 1, 0)
                norm2(i, 3, pre)
                x2_copy(i, 2)
                if pre:
                    q_high(i + 1, 1)
                x2_copy(i, 3)
                if pre:
                    q_high(i + 1, 2)
                    q_high(i + 1, 3)
                if pre:
                    mT_copy(i + 1)
                for c in range(C):
                    mix_high(i, buf3, c, xk32, xk_mixed, xk_hi)

            step(0, False, True)
            with act.Fori(1, BLOCKS - 1) as i:
                step(i, True, True)
            step(BLOCKS - 1, True, False)
            for c in range(C):
                mix_high(BLOCKS - 1, buf2, c, diff, xr_mixed, xr_hi)
            for c in range(C):
                relu_squared(BLOCKS - 1, c)
            for t in range(TT):
                tanh_r(BLOCKS - 1, t)

        @block.vector
        def _(dve):
            def low(dst, src, hi, done):
                nc.vector.tensor_tensor(dst, src, hi.bitcast(F32), ALU.subtract).then_inc(done, 1)

            dve.wait_ge(heads_ready, 1)
            nc.vector.tensor_copy(negsel[:, :, :].rearrange("p h s -> p (h s)"), th[:, :]).then_inc(dve_small, 1)

            def weight_low(units):
                for u in units:
                    dve.wait_ge(w_hi, u + 1)
                    wT, cols = weights[u // C][1], slice(P * (u % C), P * (u % C) + P)
                    low(wT[:, LO, :, cols], g_bank[u % 3][:, :].rearrange("p (c n) -> p c n", c=C), wT[:, HI, :, cols], w_lo)

            def ctx_low(item):
                for m in range(TILES[item]):
                    cols = slice(COLUMN[item] + P * m, COLUMN[item] + P * m + P)
                    dve.wait_ge(ctx_hi, FIRST_TILE[item] + m + 1)
                    low(buf3[:, LO, :, cols], ctx_bank[m][:, :].rearrange("p (c n) -> p c n", c=C), buf3[:, HI, :, cols], ctx_lo)

            def keys_low(item):
                cols = slice(COLUMN[item], COLUMN[item] + P * TILES[item])
                for g in range(G):
                    u = FIRST_UNIT[item] + g
                    dve.wait_ge(kv_hi, u + 1)
                    low(buf4[:, LO, g, cols], s_bank[u % 3][:, 0:P * TILES[item]], buf4[:, HI, g, cols], kv_lo)

            def values_low(item):
                for m in range(TILES[item]):
                    u, v = FIRST_UNIT[item] + G + m, v_place(item, m)
                    dve.wait_ge(kv_hi, u + 1)
                    if item == 0:
                        nc.vector.scalar_tensor_tensor(v[:, LO, :], s_bank[u % 3][:, :], mask[:, :], v[:, HI, :],
                                                       ALU.mult, ALU.subtract).then_inc(kv_lo, 1)
                    else:
                        nc.vector.tensor_tensor(v[:, LO, :], s_bank[u % 3][:, :], v[:, HI, :], ALU.subtract).then_inc(kv_lo, 1)

            def moments(which, i, t, src):
                n = i * TT + t + 1
                nc.vector.bn_stats(stats[:, which, t, :], src).then_inc(bn_ready[which], 1)
                dve.wait_ge(bn_ready[which], n)
                nc.vector.tensor_tensor(nm[:, which, t:t + 1], stats[:, which, t, 1:2], stats[:, which, t, 4:5], ALU.add).then_inc(sum_ready[which], 1)
                nc.vector.bn_aggr(mv[:, which, t, :], stats[:, which, t, :]).then_inc(aggr_ready[which], 1)
                dve.wait_ge(aggr_ready[which], n)
                dve.wait_ge(sum_ready[which], n)
                nc.vector.tensor_scalar(nm[:, which, t:t + 1], nm[:, which, t:t + 1], -0.5, None, ALU.mult).then_inc(mean_ready[which], 1)

            def moments1(i, t, first=False):
                dve.wait_ge(xa_loaded[t], 16 * (i + 1))
                moments(0, i, t, x_tile(t, first))

            weight_low(range(2 * C))
            ctx_low(0)
            keys_low(0)
            dve.wait_ge(tails_ready, 1)
            nc.vector.reduce_max(mask[:, :], mx[:, 0, 0:B], AX.X).then_inc(mask_ready, 1)
            ctx_low(1)
            values_low(0)
            weight_low(range(2 * C, EARLY_UNITS))
            keys_low(1)
            ctx_low(2)
            values_low(1)
            for t in range(2):
                moments1(0, t, True)
            keys_low(2)
            for t in range(2, TT):
                moments1(0, t, True)
            values_low(2)
            dve.wait_ge(gates_ready, 1)
            nc.vector.tensor_scalar(gate[:, 2:3], gate_tanh[:, 0:1], 1.0, None, ALU.mult).then_inc(dve_small, 1)
            nc.vector.tensor_scalar(gate[:, 3:4], gate_tanh[:, 1:2], 0.5, None, ALU.mult).then_inc(dve_small, 1)
            dve.wait_ge(dve_small, 3)
            dve.wait_ge(consts_ready, 1)
            dve.wait_ge(small_loaded, 64)

            def xT_low(i, t):
                dve.wait_ge(xT_hi, i * TT + t + 1)
                cols = slice(P * t, P * t + P)
                src = xT_bank[t][:, :].rearrange("p (c n) -> p c n", c=C)
                nc.vector.tensor_tensor(buf1[:, LO, :, cols], src, buf1[:, HI, :, cols].bitcast(F32), ALU.subtract).then_inc(xT_lo, 1)

            def reduce_max(i, n):
                if n == 0:
                    later(dve, mT_done, i)
                dve.wait_ge(max_done, i * MAX_UNITS + n + 1)
                g, t = n // (TT + 1), n % (TT + 1)
                if t < TT:
                    nc.vector.reduce_max(mm[:, t, 4 * g:4 * g + 4], max_bank[n][:, :].rearrange("p (h s) -> p h s", h=4), AX.X).then_inc(reduced, 1)
                else:
                    nc.vector.reduce_max(mx[:, :, 4 * g:4 * g + 4], max_bank[n][:, :].rearrange("p (t h s) -> p t h s", t=TT, h=4), AX.X).then_inc(reduced, 1)

            def whole_max(i):
                dve.wait_ge(reduced, (i + 1) * MAX_UNITS)
                nc.vector.tensor_tensor(mm[:, :, 0:H], mm[:, :, 0:H], mx[:, :, :], ALU.max).then_inc(mm_ready, 1)

            def p_low(i, g, n):
                dve.wait_ge(p_full, i * 5 * G + 5 * g + n + 1)
                nc.vector.tensor_tensor(pq[:, n, LO, :], p32[(5 * g + n) % 2], pq[:, n, HI, :], ALU.subtract).then_inc(p_lo, 1)

            def attend(i, g):
                dve.wait_ge(av_done, i * G + g + 1)
                if g:
                    dve.wait_ge(attn_lo, i * G + g)
                else:
                    dve.wait_ge(q_lo, (i + 1) * G)
                nc.vector.reciprocal(tmp[:, 0, :], d_bank[:, :]).then_inc(recip_ready, 1)
                dve.wait_ge(recip_ready, i * G + g + 1)
                nc.vector.tensor_tensor(tmp[:, 0, :], o_bank[:, :], tmp[:, 0, :], ALU.mult).then_inc(attn32_ready, 1)

            def output(i, t):
                dve.wait_ge(th_ready, i * TT + t + 1)
                dve.wait_ge(v_done, i * TT + t + 1)
                nc.vector.scalar_tensor_tensor(th[:, :], th[:, :], 1.0, g_bank[V_BANK[t]][:, :], ALU.add, ALU.mult).then_inc(u_ready, 1)
                dve.wait_ge(u_ready, i * TT + t + 1)
                nc.vector.scalar_tensor_tensor(x1[:, t, :], th[:, :], gate[:, 3:4], x1[:, t, :], ALU.mult, ALU.add).then_inc(out_ready, 1)

            def residual(i, t):
                dve.wait_ge(x1_loaded[t], 16 * (i + 1))
                dve.wait_ge(wo_done, i * TT + t + 1)
                nc.vector.scalar_tensor_tensor(x1[:, t, :], g_bank[WO_BANK[t]][:, :], gate[:, 2:3], x1[:, t, :], ALU.mult, ALU.add).then_inc(x1_ready, 1)
                dve.wait_ge(x1_ready, i * TT + t + 1)
                moments(1, i, t, x1[:, t, :])

            def first_column(i):
                dve.wait_ge(av_done, (i + 1) * G)
                dve.wait_ge(p_lo, (i + 1) * 5 * G)
                later(dve, carry_ready, i)
                nc.vector.tensor_scalar(x2[:, :, 0], carry[:, :], flag[:, bass.ds(i, 1)], None, ALU.mult).then_inc(x2_first, 1)

            def keep_carry(i):
                dve.wait_ge(x2_ready, (i + 1) * TT)
                dve.wait_ge(x2_first, i + 1)
                nc.vector.tensor_copy(carry[:, :], x2[:, :, N]).then_inc(carry_ready, 1)

            def mix_k(i, c, pre):
                dve.wait_ge(diff_ready, i * C + c + 1)
                if c == 2 and pre:
                    dve.wait_ge(xT_done, (i + 2) * TT)
                if c == 3:
                    dve.wait_ge(*((q_lo, (i + 2) * G) if pre else (attn_lo, (i + 1) * G)))
                nc.vector.scalar_tensor_tensor(xk32[c], diff[c], mu[:, 1, c:c + 1], x2[:, c, 0:N], ALU.mult, ALU.add).then_inc(xk_mixed, 1)

            def mix_r(i, c):
                dve.wait_ge(xk_mixed, i * C + c + 1)
                nc.vector.scalar_tensor_tensor(diff[c], diff[c], mu[:, 0, c:c + 1], x2[:, c, 0:N], ALU.mult, ALU.add).then_inc(xr_mixed, 1)

            def mix_low(i, dst, c, src, hi_ready, lo_ready):
                dve.wait_ge(hi_ready, i * C + c + 1)
                low(dst[:, LO, c, :], src[c], dst[:, HI, c, :], lo_ready[1])

            def xk(i, pre):
                mix_k(i, 0, pre)
                if not pre:
                    mix_low(i, buf3, 0, xk32, xk_hi, xk_lo)
                mix_k(i, 1, pre)
                mix_k(i, 2, pre)
                if pre:
                    mix_low(i, buf3, 0, xk32, xk_hi, xk_lo)
                mix_k(i, 3, pre)
                mix_low(i, buf3, 3, xk32, xk_hi, xk_lo)

            def xr(i):
                for c in range(C):
                    mix_r(i, c)
                for c in (0, 3):
                    mix_low(i, buf2, c, diff, xr_hi, xr_lo)

            for t in range(TT):
                xT_low(0, t)
            for n in range(MAX_UNITS):
                reduce_max(0, n)
            whole_max(0)

            def step(i, ffn, pre):
                if ffn:
                    xr(i - 1)
                else:
                    weight_low(late_units(0))
                for n in range(5):
                    p_low(i, 0, n)
                if not ffn:
                    weight_low(late_units(1))
                if ffn:
                    dve.wait_ge(k2_lo, i * C)
                for g in range(1, G):
                    p_low(i, g, 0)
                    p_low(i, g, 1)
                    p_low(i, g, 2)
                    attend(i, g - 1)
                    p_low(i, g, 3)
                    p_low(i, g, 4)
                    if ffn:
                        output(i - 1, g - 1)
                    else:
                        weight_low(late_units(1 + g))
                    if pre:
                        moments1(i + 1, g - 1)
                attend(i, G - 1)
                if ffn:
                    output(i - 1, TT - 1)
                else:
                    weight_low(late_units(1 + G))
                first_column(i)
                if pre:
                    for t in range(3):
                        xT_low(i + 1, t)
                    moments1(i + 1, 3)
                for t in range(TT):
                    if t == TT - 1 and pre:
                        xT_low(i + 1, 3)
                    residual(i, t)
                if pre:
                    for n in range(MAX_UNITS):
                        reduce_max(i + 1, n)
                    whole_max(i + 1)
                keep_carry(i)
                xk(i, pre)

            step(0, False, True)
            with dve.Fori(1, BLOCKS - 1) as i:
                step(i, True, True)
            step(BLOCKS - 1, True, False)
            xr(BLOCKS - 1)
            for t in range(TT):
                output(BLOCKS - 1, t)

        @block.tensor
        def _(pe):
            def product(dst, stationary, moving, chunks, before=None):
                for c in range(chunks):
                    if before:
                        before(c)
                    for n, (s, m) in enumerate(PRODUCTS):
                        ins = nc.tensor.matmul(dst, stationary(s, c), moving(m, c), start=(c, n) == (0, 0),
                                               stop=(c, n) == (chunks - 1, len(PRODUCTS) - 1))
                return ins

            def transposed(dst, tiles):
                for n, tile in enumerate(tiles):
                    ins = nc.tensor.transpose(dst[:, P * n:P * n + P], tile, ident[:, :])
                return ins

            def cols(n):
                return slice(P * n, P * n + P)

            def weights_transposed(units):
                for u in units:
                    pe.wait_ge(nat_loaded[nat_place(u)], 16 * nat_loads(u))
                    if EARLY_UNITS <= u < EARLY_UNITS + 3:
                        pe.wait_ge(q_copied, 2 + u - EARLY_UNITS)
                    elif u >= 3:
                        pe.wait_ge(w_lo, u - 2)
                    transposed(g_bank[u % 3], [nat(u)[:, cols(c)] for c in range(C)]).then_inc(w_transposed, 1)

            def ctx_transposes(item):
                pe.wait_ge(ctx_loaded, 16 * (B, B + 2, B + 4)[item])
                later(pe, ctx_lo, FIRST_TILE[item])
                for m in range(TILES[item]):
                    transposed(ctx_bank[m], [ctx_nat[:, m, cols(c)] for c in range(C)]).then_inc(ctx_transposed, 1)

            def keys(item):
                first, width = COLUMN[item], P * TILES[item]
                pe.wait_ge(ctx_lo, FIRST_TILE[item] + TILES[item])
                for g in range(G):
                    u = FIRST_UNIT[item] + g
                    later(pe, kv_lo, u - 2)
                    product(s_bank[u % 3][:, 0:width], lambda s, c: buf1[:, s, c, cols(g)],
                            lambda m, c: buf3[:, m, c, first:first + width], C).then_inc(kv_done, 1)

            def context_values(item):
                for m in range(TILES[item]):
                    u, rows = FIRST_UNIT[item] + G + m, slice(COLUMN[item] + P * m, COLUMN[item] + P * m + P)
                    pe.wait_ge(kv_lo, u - 2)
                    product(s_bank[u % 3][:, :], lambda s, c: buf3[:, s, c, rows], lambda m, c: buf2[:, m, c, :],
                            C).then_inc(kv_done, 1)

            pe.wait_ge(ident_ready, 1)
            weights_transposed(range(2 * C))
            ctx_transposes(0)
            pe.wait_ge(w_lo, 2 * C)
            keys(0)
            ctx_transposes(1)
            context_values(0)
            weights_transposed(range(2 * C, EARLY_UNITS))
            keys(1)
            ctx_transposes(2)
            context_values(1)
            keys(2)
            context_values(2)

            def xT(i, t, first=False):
                pe.wait_ge(xn1_ready, i * TT + t + 1)
                transposed(xT_bank[t], [x_tile(t, first)[:, cols(c)] for c in range(C)]).then_inc(xT_done, 1)

            def maximum(i, n):
                g, t = n // (TT + 1), n % (TT + 1)
                if n == 0:
                    pe.wait_ge(kv_loaded, 16 * KV_LOADS * (i + 1))
                if t == 0:
                    pe.wait_ge(q_hi, i * G + g + 1)
                if n >= 3:
                    pe.wait_ge(reduced, i * MAX_UNITS + n - 2)
                else:
                    later(pe, p_full, i * SCORE_UNITS)
                bank = max_bank[n]
                if t < TT:
                    ins = nc.tensor.matmul(bank[:, :], buf4[:, HI, g, cols(t)], k_pad[:, HI, g, :, :].rearrange("p j s -> p (j s)"),
                                           start=True, stop=True)
                else:
                    for e in range(TT):
                        ins = nc.tensor.matmul(bank[:, cols(e)], buf4[:, HI, g, cols(e)],
                                               k_tail[:, HI, g, :, :].rearrange("p j s -> p (j s)"), start=True, stop=True)
                ins.then_inc(max_done, 1)

            def query(i, g):
                def before(c):
                    if g:
                        for n in ((), (0, 1), (2,), (3,), (4,))[c]:
                            maximum(i, (TT + 1) * (g - 1) + n)

                if g == 0:
                    pe.wait_ge(xT_lo, (i + 1) * TT)
                product(g_bank[Q_BANK[g]][:, :], lambda s, c: WqT[:, s, c, cols(g)], lambda m, c: buf1[:, m, c, :], C,
                        before).then_inc(q_done, 1)
                before(C)

            def maxima_left(i):
                for n in range((TT + 1) * (G - 1), MAX_UNITS):
                    maximum(i, n)
                    if n == MAX_UNITS - 4:
                        pe.wait_ge(q_lo, i * G + 1)
                        later(pe, x2_ready, i * TT)
                        score(i, 0, 0)

            def maxima_transposed(i):
                pe.wait_ge(mm_ready, i + 1)
                later(pe, x2_ready, i * TT - 1)
                transposed(mT_bank, [mm[:, t, :] for t in range(TT)]).then_inc(mT_done, 1)

            def score(i, g, n):
                for k, (s, q) in enumerate(PRODUCTS):
                    keys = k_pad[:, s, g, n, :] if n < 4 else k_tail[:, s, g, :, :].rearrange("p j s -> p (j s)")
                    nc.tensor.matmul(score_bank[5 * g + n][:, :], keys, buf4[:, q, g, :], start=k == 0, stop=False)

            def less_maximum(g, n):
                if n < 4:
                    shift = negsel[:, 4 * g + n, 0:1].to_broadcast([P, P])
                else:
                    shift = negsel[:, 4 * g:4 * g + 4, :].rearrange("p h s -> p (h s)")
                nc.tensor.matmul(score_bank[5 * g + n][:, :], shift, mT[:, :], start=False, stop=True).then_inc(scores_done, 1)

            def first_scores(i):
                for n in (1, 2):
                    pe.wait_ge(reduced, (i + 1) * MAX_UNITS - 3 + n)
                    score(i, 0, n)
                maxima_transposed(i)
                score(i, 0, 3)
                pe.wait_ge(mT_ready, i + 1)
                for n in range(4):
                    less_maximum(0, n)

            def scores(i, g, units):
                pe.wait_ge(q_lo, i * G + g + 1)
                for n in units:
                    pe.wait_ge(p_full, i * SCORE_UNITS + 5 * g + n - 2)
                    score(i, g, n)
                    less_maximum(g, n)

            def values(i, g):
                pe.wait_ge(p_lo, i * SCORE_UNITS + 5 * g + 5)
                later(pe, attn32_ready, i * G + g)
                if g == 0:
                    later(pe, x2_ready, i * TT)
                for n in range(2):
                    for k, (s, q) in enumerate(PRODUCTS):
                        for j in range(4):
                            v = v_main[:, s, DH * (4 * g + j):DH * (4 * g + j + 1)] if n == 0 else v_tail[:, s, g, j, :]
                            nc.tensor.matmul(o_bank[DH * j:DH * j + DH, :], v, pq[:, 4 if n else j, q, :],
                                             start=(n, k) == (0, 0), stop=(n, k) == (1, 2))
                for n in range(2):
                    for q in (HI, LO):
                        for j in range(4):
                            one = ones_main[:, :] if n == 0 else ones_tail[:, j, :]
                            ins = nc.tensor.matmul(d_bank[DH * j:DH * j + DH, :], one, pq[:, 4 if n else j, q, :],
                                                   start=(n, q) == (0, HI), stop=(n, q) == (1, LO))
                ins.then_inc(av_done, 1)

            def project(i, t):
                def whole(c):
                    if t == 0:
                        pe.wait_ge(attn_lo, i * G + c + 1)

                product(g_bank[WO_BANK[t]][:, :], lambda s, c: buf3[:, s, c, cols(t)], lambda m, c: WoT[:, m, c, :], C, whole).then_inc(wo_done, 1)

            def x2_transposed(i, t):
                pe.wait_ge(xn2_ready, i * TT + t + 1)
                if t < 2:
                    pe.wait_ge(attn32_ready, (i + 1) * G)
                else:
                    pe.wait_ge(x2_ready, i * TT + t - 1)
                transposed(x2_bank[t], [xa[:, 1 + t % 2, cols(c)] for c in range(C)]).then_inc(x2_done, 1)

            def ffn_k(i, outs, queries=True):
                for c in outs:
                    if c == 3:
                        pe.wait_ge(relu_ready, i * C + 1)
                    elif queries:
                        pe.wait_ge(q_copied, (i + 1) * G + c + 2)
                for e in range(C):
                    wait_lo(pe, xk_lo, i, e)
                    for c in outs:
                        for n, (s, m) in enumerate(PRODUCTS):
                            ins = nc.tensor.matmul(g_bank[K_BANK[c]][:, :], WkT2[:, s, e, cols(c)], buf3[:, m, e, :],
                                                   start=(e, n) == (0, 0), stop=(e, n) == (C - 1, len(PRODUCTS) - 1))
                        if e == C - 1:
                            ins.then_inc(k_done, 1)

            def ffn_r(i, t):
                if t == 0:
                    wait_lo(pe, xr_lo, i, 2)
                    wait_lo(pe, xr_lo, i, 3)
                pe.wait_ge(*((relu_ready, i * C + 2), (relu_ready, i * C + 4), (u_ready, i * TT + 1), (u_ready, i * TT + 2))[t])
                product(g_bank[R_BANK[t]][:, :], lambda s, c: buf2[:, s, c, cols(t)], lambda m, c: WrT[:, m, c, :], C).then_inc(r_done, 1)

            def ffn_v(i, t):
                if t == 0:
                    pe.wait_ge(k2_lo, (i + 1) * C)
                pe.wait_ge(*((relu_ready, i * C + 3), (th_ready, i * TT + 1), (th_ready, i * TT + 2), (th_ready, i * TT + 3))[t])
                product(g_bank[V_BANK[t]][:, :], lambda s, c: buf1[:, s, c, cols(t)], lambda m, c: WvT2[:, m, c, :], C).then_inc(v_done, 1)

            pe.wait_ge(kv_lo, KV_UNITS)
            pe.wait_ge(w_lo, EARLY_UNITS)
            for t in range(TT):
                xT(0, t, True)
            for g in range(G):
                if g == 3:
                    pe.wait_ge(q_copied, 1)
                query(0, g)
            maxima_left(0)

            def step(i, ffn, pre):
                if not ffn:
                    weights_transposed(late_units(0))
                first_scores(i)
                if ffn:
                    ffn_k(i - 1, (0, 1, 2))
                scores(i, 0, (4,))
                scores(i, 1, (0,))
                if ffn:
                    ffn_k(i - 1, (3,))
                else:
                    weights_transposed(late_units(1))
                for g in range(1, G):
                    scores(i, g, (1, 2) if g == 1 else (0, 1, 2))
                    values(i, g - 1)
                    if ffn:
                        ffn_r(i - 1, g - 1)
                    scores(i, g, (3, 4))
                    if ffn:
                        ffn_v(i - 1, g - 1)
                    else:
                        weights_transposed(late_units(1 + g))
                if ffn:
                    ffn_r(i - 1, TT - 1)
                values(i, G - 1)
                if ffn:
                    ffn_v(i - 1, TT - 1)
                else:
                    weights_transposed(late_units(1 + G))
                if pre:
                    for t in range(3):
                        xT(i + 1, t)
                for t in range(TT):
                    if t < 3 and ffn:
                        pe.wait_ge(*((u_ready, i * TT - 1), (th_ready, i * TT), (u_ready, i * TT))[t])
                    elif t == 0:
                        pe.wait_ge(w_lo, ALL_UNITS)
                    if t == 3:
                        if pre:
                            pe.wait_ge(x1_ready, i * TT + 1)
                            xT(i + 1, 3)
                        pe.wait_ge(x1_ready, i * TT + 2)
                    project(i, t)
                x2_transposed(i, 0)
                x2_transposed(i, 1)
                for g in range(G):
                    if pre:
                        pe.wait_ge(*((x1_ready, i * TT + 3), (xT_lo, (i + 2) * TT), (x1_ready, i * TT + 4), (q_copied, (i + 1) * G + 1))[g])
                        query(i + 1, g)
                    if g < 2:
                        x2_transposed(i, 2 + g)
                if pre:
                    maxima_left(i + 1)

            step(0, False, True)
            with pe.Fori(1, BLOCKS - 1) as i:
                step(i, True, True)
            step(BLOCKS - 1, True, False)
            pe.wait_ge(x1_ready, BLOCKS * TT)
            ffn_k(BLOCKS - 1, (0, 1, 2), queries=False)
            ffn_k(BLOCKS - 1, (3,))
            for part, t in ((ffn_r, 0), (ffn_r, 1), (ffn_v, 0), (ffn_v, 1), (ffn_r, 2), (ffn_v, 2), (ffn_r, 3), (ffn_v, 3)):
                part(BLOCKS - 1, t)


NAMES = ("x", "ctx_1024", "g_xattn", "g_ffn", "L0_xattn_Wq", "L0_xattn_Wk", "L0_xattn_Wv", "L0_xattn_Wo",
         "L0_ffn_W_r", "L0_ffn_W_k", "L0_ffn_W_v", "L0_ffn_mu_r", "L0_ffn_mu_k")


def kernel(**inputs):
    import numpy as np
    import concourse.bacc as bacc
    from concourse.bass_utils import run_bass_kernel_spmd

    nc = bacc.Bacc("TRN2", target_bir_lowering=False, num_devices=1)
    arrays, args = {}, []
    for name in NAMES:
        a = np.ascontiguousarray(inputs[name])
        arrays[f"in_{name}"] = a
        args.append(nc.dram_tensor(f"in_{name}", a.shape, mybir.dt.from_np(a.dtype), kind="ExternalInput").ap())
    out = nc.dram_tensor("out_0", arrays["in_x"].shape, F32, kind="ExternalOutput").ap()
    flamingo_block(nc, *args, out)
    return run_bass_kernel_spmd(nc, [arrays], core_ids=[0]).results[0]["out_0"]
```
